# Optimizing a Trainium2 kernel written in Bass

```python
import numpy as np
import jax
import jax.numpy as jnp

def _softmax(x, axis=-1):
    return jax.nn.softmax(x, axis=axis)

def _gelu(x):
    return jax.nn.gelu(x, approximate=True)

def _silu(x):
    return jax.nn.silu(x)

def _sigmoid(x):
    return jax.nn.sigmoid(x)

def _layernorm(x, axis=-1, eps=1e-05):
    m = jnp.mean(x, axis=axis, keepdims=True)
    v = jnp.var(x, axis=axis, keepdims=True)
    return (x - m) / jnp.sqrt(v + eps)

def _scatter_add(tgt, idx, src, axis=0):
    return tgt.at[idx].add(src)

def _segment_sum(src, seg, n):
    return jax.ops.segment_sum(src, seg, n)
kernel_name = 'mk_recurrent_d1_jaxref_r8_d2e35d'

def setup_inputs(seed: int=0):
    np.random.seed(seed)
    _w = jnp.asarray

    def _L0_attn_setup():
        import math
        import jax, jax.numpy as jnp
        import numpy as np
        HID = 128
        H = 8
        D = HID // H
        CHUNK = 12
        PAST = 13 - 1
        FUT = 0
        CTX = CHUNK + PAST + FUT
        SOFTCAP = 50.0
        Q_SCALE = D ** (-0.5) / math.log(2)
        K_SCALE = math.log(1.0 + math.e) / math.log(2)

        def _extract_block_context(x, num_blocks):
            xp = jnp.pad(x, ((0, 0), (PAST, FUT + CHUNK - 1), (0, 0), (0, 0)))
            idx = jnp.arange(num_blocks)[:, None] * CHUNK + jnp.arange(CTX)[None, :]
            return xp[:, idx]

        def _rel_shift(x):
            B, Hh, nb, bs, pos_len = x.shape
            x = jnp.pad(x, ((0, 0), (0, 0), (0, 0), (0, 0), (0, CTX + 1 - pos_len)))
            x = x.reshape(B, Hh, nb, bs * (CTX + 1))[..., :bs * CTX]
            return x.reshape(B, Hh, nb, bs, CTX)
        key = jax.random.key(seed)
        ks = jax.random.split(key, 8)
        B, S = (4, 768)
        P = CTX + 1
        std = HID ** (-0.5)
        return {'hidden_states': jax.random.normal(ks[0], (B, S, HID), jnp.float32), 'position_embeddings': jax.random.normal(ks[1], (P, HID), jnp.float32), 'Wq': jax.random.normal(ks[2], (HID, HID), jnp.float32) * std, 'Wk': jax.random.normal(ks[3], (HID, HID), jnp.float32) * std, 'Wv': jax.random.normal(ks[4], (HID, HID), jnp.float32) * std, 'Wpost': jax.random.normal(ks[5], (HID, HID), jnp.float32) * std, 'Wrel': jax.random.normal(ks[6], (HID, HID), jnp.float32) * std, 'per_dim_scale': jnp.zeros((D,), jnp.float32)}
    _L0_attn_in = _L0_attn_setup()

    def _L0_ffn_setup():
        import jax, jax.numpy as jnp
        import numpy as np
        DIM = 128
        DEPTH = 6
        HEADS = 16
        DIM_HEAD = 64
        WINDOW = 32
        INNER = HEADS * DIM_HEAD
        DIM_INNER = int(DIM * 4 * 2 / 3)
        QK_SCALE = 8.0

        def shift_tokens(t):
            a, s = jnp.split(t, 2, -1)
            s = jnp.pad(s, ((0, 0), (1, 0), (0, 0)))[:, :-1]
            return jnp.concatenate([a, s], -1)

        def l2norm(t):
            return t / jnp.maximum(jnp.linalg.norm(t, axis=-1, keepdims=True), 1e-12)

        def rotate_half(x):
            x1, x2 = jnp.split(x, 2, -1)
            return jnp.concatenate([-x2, x1], -1)

        def rotary_tables(n):
            half = jnp.arange(0, DIM_HEAD, 2, dtype=jnp.float32)
            inv_freq = 1.0 / 10000.0 ** (half / DIM_HEAD)
            t = jnp.arange(n, dtype=jnp.float32)
            freqs = t[:, None] * inv_freq[None, :]
            freqs = jnp.concatenate([freqs, freqs], -1)
            base_scale = (half + 0.4 * DIM_HEAD) / (1.4 * DIM_HEAD)
            power = (t - n // 2) / (WINDOW // 2)
            scale = base_scale[None, :] ** power[:, None]
            scale = jnp.concatenate([scale, scale], -1)
            return (freqs, scale)

        def local_attention(q, k, v):
            b, h, n, d = q.shape
            w = WINDOW
            nw = n // w
            bq = q.reshape(b, h, nw, w, d)
            bk = k.reshape(b, h, nw, w, d)
            bv = v.reshape(b, h, nw, w, d)

            def look(t):
                p = jnp.pad(t, ((0, 0), (0, 0), (1, 0), (0, 0), (0, 0)))
                return jnp.concatenate([p[:, :, :nw], p[:, :, 1:]], axis=3)
            bk2, bv2 = (look(bk), look(bv))
            seq = jnp.arange(n).reshape(nw, w)
            seq_p = jnp.pad(seq, ((1, 0), (0, 0)), constant_values=-1)
            jt = jnp.concatenate([seq_p[:nw], seq_p[1:]], axis=1)
            it = seq[:, :, None]
            jb = jt[:, None, :]
            mask = (it < jb) | (it > jb + w) | (jb == -1)
            sim = jnp.einsum('bhwie,bhwje->bhwij', bq, bk2) * QK_SCALE
            sim = jnp.where(mask, -jnp.finfo(sim.dtype).max, sim)
            attn = jax.nn.softmax(sim, -1)
            out = jnp.einsum('bhwij,bhwje->bhwie', attn, bv2)
            return out.reshape(b, h, n, d)

        def attn_layer(x, Wqkv, qs, ksc, Wo):
            b, n, _ = x.shape
            qkv = x @ Wqkv
            q, k, v = jnp.split(qkv, 3, -1)
            sh = lambda t: t.reshape(b, n, HEADS, DIM_HEAD).transpose(0, 2, 1, 3)
            q, k, v = (sh(q), sh(k), sh(v))
            q = l2norm(q) * qs
            k = l2norm(k) * ksc
            freqs, scale = rotary_tables(n)
            cos, sin = (jnp.cos(freqs), jnp.sin(freqs))
            q = q * cos * scale + rotate_half(q) * sin * scale
            inv = 1.0 / scale
            k = k * cos * inv + rotate_half(k) * sin * inv
            out = local_attention(q, k, v)
            out = out.transpose(0, 2, 1, 3).reshape(b, n, INNER)
            return out @ Wo

        def ffn_layer(x, g, bln, W1, b1, W2, b2):
            mu = x.mean(-1, keepdims=True)
            var = ((x - mu) ** 2).mean(-1, keepdims=True)
            xn = (x - mu) / jnp.sqrt(var + 1e-05) * g + bln
            hg = xn @ W1 + b1
            a, gate = jnp.split(hg, 2, -1)
            return a * jax.nn.gelu(gate, approximate=False) @ W2 + b2
        key = jax.random.key(seed)
        ks = jax.random.split(key, 8)
        B, N = (2, 256)
        init = lambda k, shape: jax.random.normal(k, shape, jnp.float32) * 0.02
        return {'x': jax.random.normal(ks[0], (B, N, DIM), jnp.float32), 'Wqkv': init(ks[1], (DEPTH, DIM, 3 * INNER)), 'q_scale': jnp.ones((DEPTH, DIM_HEAD), jnp.float32), 'k_scale': jnp.ones((DEPTH, DIM_HEAD), jnp.float32), 'Wo': init(ks[2], (DEPTH, INNER, DIM)), 'ln_g': jnp.ones((DEPTH, DIM), jnp.float32), 'ln_b': jnp.zeros((DEPTH, DIM), jnp.float32), 'W1': init(ks[3], (DEPTH, DIM, 2 * DIM_INNER)), 'b1': jnp.zeros((DEPTH, 2 * DIM_INNER), jnp.float32), 'W2': init(ks[4], (DEPTH, DIM_INNER, DIM)), 'b2': jnp.zeros((DEPTH, DIM), jnp.float32)}
    _L0_ffn_in = _L0_ffn_setup()
    _d = {'L0_attn_hidden_states': _L0_attn_in['hidden_states'], 'L0_attn_position_embeddings': _L0_attn_in['position_embeddings'], 'L0_attn_Wq': _L0_attn_in['Wq'], 'L0_attn_Wk': _L0_attn_in['Wk'], 'L0_attn_Wv': _L0_attn_in['Wv'], 'L0_attn_Wpost': _L0_attn_in['Wpost'], 'L0_attn_Wrel': _L0_attn_in['Wrel'], 'L0_attn_per_dim_scale': _L0_attn_in['per_dim_scale'], 'L0_ffn_Wqkv': _L0_ffn_in['Wqkv'], 'L0_ffn_q_scale': _L0_ffn_in['q_scale'], 'L0_ffn_k_scale': _L0_ffn_in['k_scale'], 'L0_ffn_Wo': _L0_ffn_in['Wo'], 'L0_ffn_ln_g': _L0_ffn_in['ln_g'], 'L0_ffn_ln_b': _L0_ffn_in['ln_b'], 'L0_ffn_W1': _L0_ffn_in['W1'], 'L0_ffn_b1': _L0_ffn_in['b1'], 'L0_ffn_W2': _L0_ffn_in['W2'], 'L0_ffn_b2': _L0_ffn_in['b2']}
    _x0 = _d['L0_attn_hidden_states']
    _d['L0_attn_hidden_states'] = jax.random.normal(jax.random.fold_in(jax.random.key(seed), 1), (8, 512, 128), dtype=_x0.dtype)
    del _x0
    return _d

def reference(L0_attn_hidden_states, L0_attn_position_embeddings, L0_attn_Wq, L0_attn_Wk, L0_attn_Wv, L0_attn_Wpost, L0_attn_Wrel, L0_attn_per_dim_scale, L0_ffn_Wqkv, L0_ffn_q_scale, L0_ffn_k_scale, L0_ffn_Wo, L0_ffn_ln_g, L0_ffn_ln_b, L0_ffn_W1, L0_ffn_b1, L0_ffn_W2, L0_ffn_b2):

    def _L0_attn_ref(hidden_states, position_embeddings, Wq, Wk, Wv, Wpost, Wrel, per_dim_scale):
        import math
        import jax, jax.numpy as jnp
        import numpy as np
        HID = 128
        H = 8
        D = HID // H
        CHUNK = 12
        PAST = 13 - 1
        FUT = 0
        CTX = CHUNK + PAST + FUT
        SOFTCAP = 50.0
        Q_SCALE = D ** (-0.5) / math.log(2)
        K_SCALE = math.log(1.0 + math.e) / math.log(2)

        def _extract_block_context(x, num_blocks):
            xp = jnp.pad(x, ((0, 0), (PAST, FUT + CHUNK - 1), (0, 0), (0, 0)))
            idx = jnp.arange(num_blocks)[:, None] * CHUNK + jnp.arange(CTX)[None, :]
            return xp[:, idx]

        def _rel_shift(x):
            B, Hh, nb, bs, pos_len = x.shape
            x = jnp.pad(x, ((0, 0), (0, 0), (0, 0), (0, 0), (0, CTX + 1 - pos_len)))
            x = x.reshape(B, Hh, nb, bs * (CTX + 1))[..., :bs * CTX]
            return x.reshape(B, Hh, nb, bs, CTX)
        B, S, _ = hidden_states.shape
        nb = (S + CHUNK - 1) // CHUNK
        pad = nb * CHUNK - S
        q = (hidden_states @ Wq.T).reshape(B, S, H, D)
        k = (hidden_states @ Wk.T).reshape(B, S, H, D)
        v = (hidden_states @ Wv.T).reshape(B, S, H, D)
        q = q * (Q_SCALE * jax.nn.softplus(per_dim_scale))
        k = k * K_SCALE
        q_blocked = jnp.pad(q, ((0, 0), (0, pad), (0, 0), (0, 0))).reshape(B, nb, CHUNK, H, D)
        k_ctx = _extract_block_context(k, nb)
        v_ctx = _extract_block_context(v, nb)
        matrix_ac = jnp.einsum('bnchd,bnkhd->bhnck', q_blocked, k_ctx)
        rel_k = (position_embeddings @ Wrel.T).reshape(-1, H, D)
        matrix_bd = jnp.einsum('bnchd,phd->bhncp', q_blocked, rel_k)
        matrix_bd = _rel_shift(matrix_bd)
        logits = matrix_ac + matrix_bd
        logits = jnp.tanh(logits / SOFTCAP) * SOFTCAP
        attn = jax.nn.softmax(logits, axis=-1)
        out = jnp.einsum('bhnck,bnkhd->bnchd', attn, v_ctx)
        out = out.reshape(B, nb * CHUNK, H * D)[:, :S]
        return out @ Wpost.T

    def _L0_ffn_ref(x, Wqkv, q_scale, k_scale, Wo, ln_g, ln_b, W1, b1, W2, b2):
        import jax, jax.numpy as jnp
        import numpy as np
        DIM = 128
        DEPTH = 6
        HEADS = 16
        DIM_HEAD = 64
        WINDOW = 32
        INNER = HEADS * DIM_HEAD
        DIM_INNER = int(DIM * 4 * 2 / 3)
        QK_SCALE = 8.0

        def shift_tokens(t):
            a, s = jnp.split(t, 2, -1)
            s = jnp.pad(s, ((0, 0), (1, 0), (0, 0)))[:, :-1]
            return jnp.concatenate([a, s], -1)

        def l2norm(t):
            return t / jnp.maximum(jnp.linalg.norm(t, axis=-1, keepdims=True), 1e-12)

        def rotate_half(x):
            x1, x2 = jnp.split(x, 2, -1)
            return jnp.concatenate([-x2, x1], -1)

        def rotary_tables(n):
            half = jnp.arange(0, DIM_HEAD, 2, dtype=jnp.float32)
            inv_freq = 1.0 / 10000.0 ** (half / DIM_HEAD)
            t = jnp.arange(n, dtype=jnp.float32)
            freqs = t[:, None] * inv_freq[None, :]
            freqs = jnp.concatenate([freqs, freqs], -1)
            base_scale = (half + 0.4 * DIM_HEAD) / (1.4 * DIM_HEAD)
            power = (t - n // 2) / (WINDOW // 2)
            scale = base_scale[None, :] ** power[:, None]
            scale = jnp.concatenate([scale, scale], -1)
            return (freqs, scale)

        def local_attention(q, k, v):
            b, h, n, d = q.shape
            w = WINDOW
            nw = n // w
            bq = q.reshape(b, h, nw, w, d)
            bk = k.reshape(b, h, nw, w, d)
            bv = v.reshape(b, h, nw, w, d)

            def look(t):
                p = jnp.pad(t, ((0, 0), (0, 0), (1, 0), (0, 0), (0, 0)))
                return jnp.concatenate([p[:, :, :nw], p[:, :, 1:]], axis=3)
            bk2, bv2 = (look(bk), look(bv))
            seq = jnp.arange(n).reshape(nw, w)
            seq_p = jnp.pad(seq, ((1, 0), (0, 0)), constant_values=-1)
            jt = jnp.concatenate([seq_p[:nw], seq_p[1:]], axis=1)
            it = seq[:, :, None]
            jb = jt[:, None, :]
            mask = (it < jb) | (it > jb + w) | (jb == -1)
            sim = jnp.einsum('bhwie,bhwje->bhwij', bq, bk2) * QK_SCALE
            sim = jnp.where(mask, -jnp.finfo(sim.dtype).max, sim)
            attn = jax.nn.softmax(sim, -1)
            out = jnp.einsum('bhwij,bhwje->bhwie', attn, bv2)
            return out.reshape(b, h, n, d)

        def attn_layer(x, Wqkv, qs, ksc, Wo):
            b, n, _ = x.shape
            qkv = x @ Wqkv
            q, k, v = jnp.split(qkv, 3, -1)
            sh = lambda t: t.reshape(b, n, HEADS, DIM_HEAD).transpose(0, 2, 1, 3)
            q, k, v = (sh(q), sh(k), sh(v))
            q = l2norm(q) * qs
            k = l2norm(k) * ksc
            freqs, scale = rotary_tables(n)
            cos, sin = (jnp.cos(freqs), jnp.sin(freqs))
            q = q * cos * scale + rotate_half(q) * sin * scale
            inv = 1.0 / scale
            k = k * cos * inv + rotate_half(k) * sin * inv
            out = local_attention(q, k, v)
            out = out.transpose(0, 2, 1, 3).reshape(b, n, INNER)
            return out @ Wo

        def ffn_layer(x, g, bln, W1, b1, W2, b2):
            mu = x.mean(-1, keepdims=True)
            var = ((x - mu) ** 2).mean(-1, keepdims=True)
            xn = (x - mu) / jnp.sqrt(var + 1e-05) * g + bln
            hg = xn @ W1 + b1
            a, gate = jnp.split(hg, 2, -1)
            return a * jax.nn.gelu(gate, approximate=False) @ W2 + b2
        for i in range(DEPTH):
            x = attn_layer(shift_tokens(x), Wqkv[i], q_scale[i], k_scale[i], Wo[i]) + x
            x = ffn_layer(shift_tokens(x), ln_g[i], ln_b[i], W1[i], b1[i], W2[i], b2[i]) + x
        return x
    x = L0_attn_hidden_states
    xn = _layernorm(x, axis=-1)
    s = _L0_attn_ref(xn, L0_attn_position_embeddings, L0_attn_Wq, L0_attn_Wk, L0_attn_Wv, L0_attn_Wpost, L0_attn_Wrel, L0_attn_per_dim_scale)
    g = _silu(_L0_ffn_ref(xn, L0_ffn_Wqkv, L0_ffn_q_scale, L0_ffn_k_scale, L0_ffn_Wo, L0_ffn_ln_g, L0_ffn_ln_b, L0_ffn_W1, L0_ffn_b1, L0_ffn_W2, L0_ffn_b2))
    x = x + s * g
    return x

_drawn_inputs = setup_inputs


def setup_inputs(seed=0):
    import zlib

    import numpy as np

    out = dict(_drawn_inputs(seed))
    spreads = {'L0_attn_per_dim_scale': (0.0, 0.342),
     'L0_ffn_q_scale': (1.0, 0.6),
     'L0_ffn_k_scale': (1.0, 0.6),
     'L0_ffn_ln_g': (1.0, 0.6),
     'L0_ffn_ln_b': (0.0, 0.8),
     'L0_ffn_b1': (0.0, 0.8),
     'L0_ffn_b2': (0.0, 0.332)}
    factors = {'L0_ffn_W1': 5.673, 'L0_ffn_W2': 5.558}
    for name, (base, spread) in spreads.items():
        noise = np.random.default_rng([zlib.crc32(name.encode()), seed]).standard_normal(out[name].shape)
        drawn = base * np.exp(spread * noise) if base else spread * noise
        out[name] = jnp.asarray(drawn.astype(out[name].dtype))
    for name, factor in factors.items():
        out[name] = (out[name] * factor).astype(out[name].dtype)
    return out
```

```python
import math
from contextlib import ExitStack

import numpy as np

import concourse.bass as bass
from concourse import mybir

ALU = mybir.AluOpType
ACT = mybir.ActivationFunctionType
F32 = mybir.dt.float32
BF16 = mybir.dt.bfloat16
AX_X = mybir.AxisListType.X

P = 128
B, S, D = 8, 512, 128
TB = S // P
EPS = 1e-5

CH, CCH, CD = 8, 12, 16
CTX = 2 * CCH
NPOS = CTX + 1
NB = -(-S // CCH)
SP = NB * CCH
NTILE = -(-B * NB // P)
TW = P * CCH
SOFTCAP = 50.0
Q_SCALE = CD ** -0.5 / math.log(2)
K_SCALE = math.log(1.0 + math.e) / math.log(2)

DEPTH, HEADS, DH, WIN = 6, 16, 64, 32
INNER = HEADS * DH
HP = HEADS // 2
HALF = DH // 2
DI = int(D * 4 * 2 / 3)
NJ = -(-DI // P)
JW = [min(P, DI - P * j) for j in range(NJ)]
NEG = -1e30
RN = 256.0

C_ID, C_MASK, C_QC, C_QS, C_KC, C_KS = 0, 128, 384, 896, 1408, 1920
C_PAIR, C_MEAN, C_HM, C_PM = 2432, 2560, 2688, 2696
C_END = C_PM + NTILE


def constants():
    c = np.zeros((P, C_END), np.float32)
    c[:, C_ID:C_ID + P] = np.eye(P)
    i = np.arange(P) % WIN
    j = np.arange(2 * WIN)
    ok = (j[None] >= i[:, None]) & (j[None] <= i[:, None] + WIN)
    mask = np.tile(np.where(ok, 0.0, NEG), (1, 4)).astype(np.float32)
    mask[0:WIN, 0:WIN] = NEG
    c[:, C_MASK:C_MASK + 256] = mask
    f = np.float32
    half = np.arange(0, DH, 2, dtype=f)
    inv_freq = (f(1.0) / f(10000.0) ** (half / f(DH))).astype(f)
    t = np.arange(S, dtype=f)
    freqs = t[:, None] * inv_freq[None]
    base = (half + f(0.4 * DH)) / f(1.4 * DH)
    power = ((t - S // 2) / f(WIN // 2)).astype(f)
    scale = base[None] ** power[:, None]
    cos, sin = np.cos(freqs), np.sin(freqs)
    sign = np.where(np.arange(P) % DH < HALF, -1.0, 1.0).astype(f)[:, None]
    four = lambda a: np.tile(a.T, (4, 1)).astype(f)
    c[:, C_QC:C_QC + S] = 8 * RN * four(cos * scale)
    c[:, C_QS:C_QS + S] = 8 * RN * four(sin * scale) * sign
    c[:, C_KC:C_KC + S] = RN * four(cos / scale)
    c[:, C_KS:C_KS + S] = RN * four(sin / scale) * sign
    p = np.arange(P)
    c[:, C_PAIR:C_PAIR + P] = p[:, None] // DH == p[None] // DH
    c[:, C_MEAN:C_MEAN + P] = 1.0 / D
    c[:, C_HM:C_HM + CH] = p[:, None] // CD == np.arange(CH)[None]
    for n in range(NTILE):
        c[:, C_PM + n] = (n * P + p) % NB != 0
    return c


def build(nc, t, out):
    with ExitStack() as top:
        def sb(name, shape, dt=F32, ctx=top):
            return ctx.enter_context(nc.sbuf_tensor(name, shape, dt))

        sems = []

        def sem(name):
            sems.append(top.enter_context(nc.semaphore(name)))
            return sems[-1]

        ps = top.enter_context(nc.psum_tensor("ps", [P, 8, 512], F32))
        con = sb("con", [P, C_END])
        xT = sb("xT", [P, B, S])
        sT = sb("sT", [P, NTILE * TW])
        ident = con[:, C_ID:C_ID + P]

        d_in, d_out = sem("d_in"), sem("d_out")

        def clear():
            for s in sems:
                nc.sync.sem_clear(s)
            nc.all_engine_barrier()

        clear()

        conf = ExitStack()
        cx = sb("cx", [P, CCH + NTILE * TW], ctx=conf)
        s_zero, s_stat, s_var, s_rs, s_xn, s_tr, s_xt = (
            sem("s_zero"), sem("s_stat"), sem("s_var"), sem("s_rs"), sem("s_xn"), sem("s_tr"), sem("s_xt"))
        with ExitStack() as ctx:
            xnat = sb("xnat", [P, B, TB, D], ctx=ctx)
            stat = sb("stat", [P, TB, 6], ctx=ctx)
            mv = sb("mv", [P, TB, 2], ctx=ctx)
            lnv = sb("lnv", [P, TB], ctx=ctx)
            rstd = sb("rstd", [P, TB], ctx=ctx)
            xn = sb("xn", [P, TB, D], ctx=ctx)
            with nc.Block(no_gpsimd_drain=True) as block:
                @block.sync
                def _(sp):
                    sp.dma_start(con[:], t["consts"]).then_inc(d_in, 16)
                    sp.dma_start(xnat[:].rearrange("p b t d -> p (b t) d"),
                                 t["L0_attn_hidden_states"].rearrange("b (t p) d -> p (b t) d", p=P)).then_inc(d_in, 16)
                    sp.wait_ge(d_in, 32)

                @block.vector
                def _(dve):
                    nc.vector.memset(cx[:], 0.0).then_inc(s_zero, 1)
                    dve.wait_ge(s_zero, 1)
            clear()
            with nc.Fori(0, B) as b:
                with nc.Block(no_gpsimd_drain=True) as block:
                    @block.vector
                    def _(dve):
                        for k in range(TB):
                            nc.vector.bn_stats(stat[:, k, :], xnat[:, b, k, :]).then_inc(s_stat, 1)
                        dve.wait_ge(s_stat, TB)
                        for k in range(TB):
                            nc.vector.bn_aggr(mv[:, k, :], stat[:, k, :]).then_inc(s_stat, 1)
                        dve.wait_ge(s_stat, 2 * TB)
                        nc.vector.tensor_scalar(lnv[:], mv[:, :, 1], EPS, None, ALU.add).then_inc(s_var, 1)
                        dve.wait_ge(s_rs, 1)
                        for k in range(TB):
                            nc.vector.tensor_scalar(xn[:, k, :], xnat[:, b, k, :], mv[:, k, 0:1],
                                                    rstd[:, k:k + 1], ALU.subtract, ALU.mult).then_inc(s_xn, 1)

                    @block.scalar
                    def _(act):
                        act.wait_ge(s_var, 1)
                        nc.scalar.activation(lnv[:], lnv[:], ACT.Ln).then_inc(s_var, 1)
                        act.wait_ge(s_var, 2)
                        nc.scalar.activation(rstd[:], lnv[:], ACT.Exp, scale=-0.5).then_inc(s_rs, 1)
                        act.wait_ge(s_tr, 1)
                        nc.scalar.copy(xT[:, b, :], ps[:, 0, :]).then_inc(s_xt, 1)
                        act.wait_ge(s_xt, 1)
                        nc.scalar.copy(cx[:, bass.ds(b * SP + CCH, S)], xT[:, b, :])

                    @block.tensor
                    def _(pe):
                        for k in range(TB):
                            pe.wait_ge(s_xn, k + 1)
                            last = nc.tensor.transpose(ps[:, 0, k * P:(k + 1) * P], xn[:, k, :], ident)
                        last.then_inc(s_tr, 1)
                clear()

        with conf:
            chunked_attention(nc, t, conf, sb, sem, clear, con, ident, ps, cx, sT)

        with ExitStack() as ctx:
            transformer(nc, t, ctx, sb, sem, clear, con, ident, ps, xT)

        s_z, s_y, s_t4, s_o = sem("s_z"), sem("s_y"), sem("s_t4"), sem("s_o")
        with ExitStack() as ctx:
            z = sb("z", [P, S], ctx=ctx)
            y = sb("y", [P, S], ctx=ctx)
            xrow = sb("xrow", [P, TB, D], ctx=ctx)
            orow = sb("orow", [P, TB, D], ctx=ctx)
            clear()
            with nc.Fori(0, B) as b:
                with nc.Block(no_gpsimd_drain=True) as block:
                    @block.sync
                    def _(sp):
                        sp.dma_start(xrow[:], t["L0_attn_hidden_states"].rearrange(
                            "b (t p) d -> p b t d", p=P)[:, b]).then_inc(d_in, 16)
                        sp.wait_ge(s_o, 1)
                        sp.dma_start(out.rearrange("b (t p) d -> p b t d", p=P)[:, b], orow[:]).then_inc(d_out, 16)
                        sp.wait_ge(d_out, 16)

                    @block.scalar
                    def _(act):
                        nc.scalar.activation(z[:], xT[:, b, :], ACT.Silu).then_inc(s_z, 1)

                    @block.vector
                    def _(dve):
                        dve.wait_ge(s_z, 1)
                        nc.vector.tensor_tensor(y[:], sT[:, bass.ds(b * SP, S)], z[:], ALU.mult).then_inc(s_y, 1)
                        dve.wait_ge(s_t4, 1)
                        dve.wait_ge(d_in, 16)
                        nc.vector.tensor_tensor(orow[:], ps[:, 0, :].rearrange("p (t d) -> p t d", t=TB),
                                                xrow[:], ALU.add).then_inc(s_o, 1)

                    @block.tensor
                    def _(pe):
                        pe.wait_ge(s_y, 1)
                        for k in range(TB):
                            last = nc.tensor.transpose(ps[:, 0, k * P:(k + 1) * P], y[:, k * P:(k + 1) * P], ident)
                        last.then_inc(s_t4, 1)
                clear()


def chunked_attention(nc, t, ctx0, sb, sem, clear, con, ident, ps, cx, sT):
    d_w, s_sp, s_ws, s_wt, s_we, s_re = (
        sem("d_w"), sem("s_sp"), sem("s_ws"), sem("s_wt"), sem("s_we"), sem("s_re"))
    with ExitStack() as ctx:
        names = ["L0_attn_Wq", "L0_attn_Wk", "L0_attn_Wv", "L0_attn_Wpost", "L0_attn_Wrel"]
        wnat = sb("wnat", [P, 5, P], ctx=ctx)
        pos = sb("pos", [NPOS, P], ctx=ctx)
        pds = sb("pds", [P, 6], ctx=ctx)
        wqs = sb("wqs", [P, P], ctx=ctx)
        wrelT = sb("wrelT", [P, P], ctx=ctx)
        posT = sb("posT", [P, NPOS], ctx=ctx)
        relT = sb("relT", [P, NPOS], ctx=ctx)
        relE = sb("relE", [P, CH, NPOS], ctx=ctx)
        wqkv = sb("cwqkv", [P, 3 * P], ctx=ctx)
        wqr = sb("wqr", [P, CH * NPOS], ctx=ctx)
        wpostT = sb("wpostT", [P, P], ctx=ctx)
        clear()
        with nc.Block(no_gpsimd_drain=True) as block:
            @block.sync
            def _(sp):
                for i, n in enumerate(names):
                    sp.dma_start(wnat[:, i, :], t[n]).then_inc(d_w, 16)
                sp.dma_start(pos[:], t["L0_attn_position_embeddings"]).then_inc(d_w, 16)
                for h in range(CH):
                    sp.dma_start(pds[h * CD:(h + 1) * CD, 0:1],
                                 t["L0_attn_per_dim_scale"].rearrange("(d o) -> d o", o=1)).then_inc(d_w, 16)

            @block.vector
            def _(dve):
                dve.wait_ge(d_w, 16 * (6 + CH))
                nc.vector.scalar_tensor_tensor(out=pds[:, 1:2], in0=pds[:, 0:1], scalar=-1.0, in1=pds[:, 0:1],
                                               op0=ALU.mult, op1=ALU.min).then_inc(s_sp, 1)
                dve.wait_ge(s_sp, 2)
                nc.vector.tensor_scalar(pds[:, 3:4], pds[:, 2:3], 1.0, None, ALU.add).then_inc(s_sp, 1)
                dve.wait_ge(s_sp, 4)
                nc.vector.scalar_tensor_tensor(out=pds[:, 5:6], in0=pds[:, 0:1], scalar=0.0, in1=pds[:, 4:5],
                                               op0=ALU.max, op1=ALU.add).then_inc(s_sp, 1)
                dve.wait_ge(s_sp, 5)
                nc.vector.tensor_scalar(wqs[:], wnat[:, 0, :], pds[:, 5:6], Q_SCALE,
                                        ALU.mult, ALU.mult).then_inc(s_ws, 1)
                dve.wait_ge(s_wt, 7)
                nc.vector.tensor_copy(relT[:], ps[:, 6, 0:NPOS]).then_inc(s_re, 1)
                dve.wait_ge(s_re, 1)
                nc.vector.tensor_tensor(relE[:], relT[:].unsqueeze(1).broadcast_to([P, CH, NPOS]),
                                        con[:, C_HM:C_HM + CH].unsqueeze(2).broadcast_to([P, CH, NPOS]),
                                        ALU.mult).then_inc(s_re, 1)
                dve.wait_ge(s_wt, 8)
                nc.vector.tensor_copy(wqr[:], ps[:, 7, 0:CH * NPOS]).then_inc(s_re, 1)

            @block.scalar
            def _(act):
                act.wait_ge(s_sp, 1)
                nc.scalar.activation(pds[:, 2:3], pds[:, 1:2], ACT.Exp).then_inc(s_sp, 1)
                act.wait_ge(s_sp, 3)
                nc.scalar.activation(pds[:, 4:5], pds[:, 3:4], ACT.Ln).then_inc(s_sp, 1)
                act.wait_ge(s_wt, 6)
                nc.scalar.copy(wqkv[:, 0:P], ps[:, 0, 0:P]).then_inc(s_we, 1)
                nc.scalar.mul(wqkv[:, P:2 * P], ps[:, 1, 0:P], K_SCALE).then_inc(s_we, 1)
                nc.scalar.copy(wqkv[:, 2 * P:], ps[:, 2, 0:P]).then_inc(s_we, 1)
                nc.scalar.copy(wpostT[:], ps[:, 3, 0:P]).then_inc(s_we, 1)
                nc.scalar.copy(wrelT[:], ps[:, 4, 0:P]).then_inc(s_we, 1)
                nc.scalar.copy(posT[:], ps[:, 5, 0:NPOS]).then_inc(s_we, 1)

            @block.tensor
            def _(pe):
                pe.wait_ge(s_ws, 1)
                nc.tensor.transpose(ps[:, 0, 0:P], wqs[:], ident).then_inc(s_wt, 1)
                for i in range(1, 5):
                    nc.tensor.transpose(ps[:, i, 0:P], wnat[:, i, :], ident).then_inc(s_wt, 1)
                nc.tensor.transpose(ps[:, 5, 0:NPOS], pos[:], ident[0:NPOS, 0:NPOS]).then_inc(s_wt, 1)
                pe.wait_ge(s_we, 6)
                nc.tensor.matmul(ps[:, 6, 0:NPOS], wrelT[:], posT[:], start=True, stop=True).then_inc(s_wt, 1)
                pe.wait_ge(s_re, 2)
                nc.tensor.matmul(ps[:, 7, 0:CH * NPOS], wqs[:], relE[:].rearrange("p h r -> p (h r)"),
                                 start=True, stop=True).then_inc(s_wt, 1)
        clear()

        ct = sb("ct", [P, CCH + TW], ctx=ctx)
        pm = sb("pm", [P, 1], ctx=ctx)
        qb = sb("qb", [P, CCH, P], ctx=ctx)
        kv = sb("kv", [P, CTX, 2, P], ctx=ctx)
        rel = sb("rel", [P, CH, CCH * NPOS], ctx=ctx)
        sc = sb("sc", [P, CH, CCH, CTX], ctx=ctx)
        NPR = 4
        prod = sb("prod", [P, NPR, CH * CTX * CD], ctx=ctx)
        sm = sb("sm", [P, CH * CCH], ctx=ctx)
        ri = sb("ri", [P, CH * CCH], ctx=ctx)
        ob = sb("ob", [P, CCH, P], ctx=ctx)
        obT = sb("obT", [P, CCH, P], ctx=ctx)
        so = sb("so", [P, P, CCH], ctx=ctx)
        s_ct, s_pj, s_ev, s_ed, s_mul, s_red, s_sc, s_sm, s_ot, s_oe, s_wp, s_so = (
            sem("s_ct"), sem("s_pj"), sem("s_ev"), sem("s_ed"), sem("s_mul"), sem("s_red"), sem("s_sc"),
            sem("s_sm"), sem("s_ot"), sem("s_oe"), sem("s_wp"), sem("s_so"))
        s_mulp = sem("s_mulp")

        def key_product(eng, c):
            return eng.tensor_tensor(
                prod[:, c % NPR, :].rearrange("p (h k d) -> p h k d", h=CH, k=CTX),
                qb[:, c, :].rearrange("p (h d) -> p h d", h=CH).unsqueeze(2).broadcast_to([P, CH, CTX, CD]),
                kv[:, :, 0, :].rearrange("p k (h d) -> p h k d", h=CH), ALU.mult)

        def value_product(eng, c):
            return eng.tensor_tensor(
                prod[:, c % NPR, :].rearrange("p (h d k) -> p h d k", h=CH, d=CD),
                sc[:, :, c, :].unsqueeze(2).broadcast_to([P, CH, CD, CTX]),
                kv[:, :, 1, :].rearrange("p k (h d) -> p h d k", h=CH), ALU.mult)

        def on_pool(c):
            return c % 2 == 1

        with nc.Fori(0, NTILE) as n:
            with nc.Block(no_gpsimd_drain=True) as block:
                @block.scalar
                def _(act):
                    nc.scalar.copy(ct[:], cx[:, bass.ds(n * TW, CCH + TW)]).then_inc(s_ct, 1)
                    for c in range(CCH):
                        act.wait_ge(s_pj, 3 * c + 1)
                        nc.scalar.copy(qb[:, c, :], ps[:, 3 * c % 6, 0:P])
                        nc.scalar.copy(kv[:, CCH + c, :, :].rearrange("p a d -> p (a d)"),
                                       ps[:, 3 * c % 6, P:3 * P]).then_inc(s_ev, 1)
                    scores = sc[:].rearrange("p h c k -> p (h c k)")
                    act.wait_ge(s_sc, 1)
                    nc.scalar.activation(scores, scores, ACT.Tanh, scale=1.0 / SOFTCAP).then_inc(s_sc, 1)
                    act.wait_ge(s_sc, 2)
                    nc.scalar.activation(scores, scores, ACT.Exp, scale=SOFTCAP).then_inc(s_sc, 1)
                    for g in range(3):
                        act.wait_ge(s_ot, g + 1)
                        nc.scalar.copy(obT[:, 4 * g:4 * g + 4, :], ps[:, g, :].rearrange("p (c m) -> p c m", c=4)) \
                           .then_inc(s_oe, 1)
                    for g in range(3):
                        act.wait_ge(s_wp, g + 1)
                        nc.scalar.copy(so[:].rearrange("p m c -> p c m")[:, 4 * g:4 * g + 4, :],
                                       ps[:, 3 + g, :].rearrange("p (c m) -> p c m", c=4)).then_inc(s_so, 1)
                    act.wait_ge(s_so, 3)
                    nc.scalar.copy(sT[:, bass.ds(n * TW, TW)], so[:].rearrange("p m c -> p (m c)")).then_inc(s_so, 1)
                    act.wait_ge(s_so, 4)

                @block.tensor
                def _(pe):
                    pe.wait_ge(s_ct, 1)
                    for c in range(CCH):
                        own = ct[:, CCH + c:CCH + c + (P - 1) * CCH + 1:CCH]
                        prev = ct[:, c:c + (P - 1) * CCH + 1:CCH]
                        if c >= 2:
                            pe.wait_ge(s_ev, c - 1)
                            pe.wait_ge(s_ed, 2 * (c - 1))
                        k = 3 * c % 6
                        nc.tensor.matmul(ps[:, k, 0:3 * P], own, wqkv[:], start=True, stop=True).then_inc(s_pj, 1)
                        nc.tensor.matmul(ps[:, k + 1, 0:CH * NPOS], own, wqr[:], start=True, stop=True).then_inc(s_pj, 1)
                        nc.tensor.matmul(ps[:, k + 2, 0:2 * P], prev, wqkv[:, P:], start=True, stop=True).then_inc(s_pj, 1)
                    pe.wait_ge(s_ev, CCH)
                    pe.wait_ge(s_ed, 2 * CCH)
                    for g in range(3):
                        pe.wait_ge(s_red, CCH + 4 * g + 4)
                        for c in range(4):
                            last = nc.tensor.transpose(ps[:, g, c * P:(c + 1) * P], ob[:, 4 * g + c, :], ident)
                        last.then_inc(s_ot, 1)
                    for g in range(3):
                        pe.wait_ge(s_oe, g + 1)
                        nc.tensor.matmul(ps[:, 3 + g, :], wpostT[:],
                                         obT[:, 4 * g:4 * g + 4, :].rearrange("p c m -> p (c m)"),
                                         start=True, stop=True).then_inc(s_wp, 1)

                @block.gpsimd
                def _(pool):
                    pool.wait_ge(s_ev, CCH)
                    pool.wait_ge(s_ed, 2 * CCH)
                    for c in range(CCH):
                        if on_pool(c):
                            if c >= NPR:
                                pool.wait_ge(s_red, c - NPR + 1)
                            key_product(nc.gpsimd, c).then_inc(s_mulp, 1)
                    pool.wait_ge(s_sc, 4)
                    for c in range(CCH):
                        if on_pool(c):
                            pool.wait_ge(s_red, CCH + c - NPR + 1)
                            value_product(nc.gpsimd, c).then_inc(s_mulp, 1)

                @block.vector
                def _(dve):
                    nc.vector.tensor_copy(pm[:], con[:, bass.ds(n + C_PM, 1)]).then_inc(s_mul, 1)
                    dve.wait_ge(s_mul, 1)
                    for c in range(CCH):
                        k = 3 * c % 6
                        dve.wait_ge(s_pj, 3 * c + 2)
                        nc.vector.tensor_copy(rel[:, :, c * NPOS:(c + 1) * NPOS],
                                              ps[:, k + 1, 0:CH * NPOS].rearrange("p (h r) -> p h r", h=CH)) \
                            .then_inc(s_ed, 1)
                        dve.wait_ge(s_pj, 3 * c + 3)
                        nc.vector.tensor_scalar(kv[:, c, :, :].rearrange("p a d -> p (a d)"),
                                                ps[:, k + 2, 0:2 * P], pm[:], None, ALU.mult).then_inc(s_ed, 1)
                    dve.wait_ge(s_ev, CCH)
                    dve.wait_ge(s_ed, 2 * CCH)
                    done = 1

                    def sums(c, view, dst):
                        nonlocal done
                        if not on_pool(c):
                            dve.wait_ge(s_mul, done)
                        nc.vector.tensor_reduce(dst, prod[:, c % NPR, :].rearrange(view, h=CH, i=dst.shape[2]),
                                                AX_X, ALU.add).then_inc(s_red, 1)

                    for c in range(CCH):
                        if on_pool(c):
                            dve.wait_ge(s_mulp, c // 2 + 1)
                        else:
                            if c >= NPR:
                                dve.wait_ge(s_red, c - NPR + 1)
                            key_product(nc.vector, c).then_inc(s_mul, 1)
                            done += 1
                        sums(c, "p (h i d) -> p h i d", sc[:, :, c, :])
                    dve.wait_ge(s_red, CCH)
                    nc.vector.tensor_tensor(sc[:].rearrange("p h c k -> p h (c k)"),
                                            sc[:].rearrange("p h c k -> p h (c k)"),
                                            rel[:, :, 0:CCH * CTX], ALU.add).then_inc(s_sc, 1)
                    dve.wait_ge(s_sc, 3)
                    rows = sc[:].rearrange("p h c k -> p (h c) k")
                    nc.vector.tensor_reduce(sm[:], rows, AX_X, ALU.add).then_inc(s_sm, 1)
                    dve.wait_ge(s_sm, 1)
                    nc.vector.reciprocal(ri[:], sm[:]).then_inc(s_sm, 1)
                    dve.wait_ge(s_sm, 2)
                    nc.vector.tensor_tensor(rows, rows, ri[:].unsqueeze(2).broadcast_to([P, CH * CCH, CTX]),
                                            ALU.mult).then_inc(s_sc, 1)
                    dve.wait_ge(s_sc, 4)
                    for c in range(CCH):
                        if on_pool(c):
                            dve.wait_ge(s_mulp, CCH // 2 + c // 2 + 1)
                        else:
                            dve.wait_ge(s_red, CCH + c - NPR + 1)
                            value_product(nc.vector, c).then_inc(s_mul, 1)
                            done += 1
                        sums(c, "p (h i k) -> p h i k", ob[:, c, :].rearrange("p (h d) -> p h d", h=CH))
            clear()


def transformer(nc, t, ctx, sb0, sem, clear, con, ident, ps, xT):
    def sb(name, shape, dt=F32):
        return sb0(name, shape, dt, ctx=ctx)

    w = sb("w", [P, 3 * INNER])
    wsw = sb("wsw", [P, 2 * INNER])
    wo = sb("wo", [P, HP, D])
    w1 = sb("w1", [P, 2 * DI])
    w2 = sb("w2", [P, NJ, D])
    vec = sb("vec", [P, 4 + 2 + 2 * NJ + 1])
    V_G, V_B, V_B1, V_B2 = 4, 5, 6, 6 + 2 * NJ
    tab = sb("tab", [P, 4, S])
    maskb = sb("maskb", [P, 256], BF16)
    identb = sb("identb", [P, P], BF16)
    xs = sb("xs", [P, WIN + S])
    v = sb("v", [P, 2, TB, INNER])
    sq = sb("sq", [P, 2, S])
    r1 = sb("r1", [P, 2, S])
    ra = sb("ra", [P, 2, S])
    rb = sb("rb", [P, 2, S])
    qn = sb("qn", [P, 2, S])
    kn = sb("kn", [P, 2, WIN + S])
    pr = sb("pr", [P, 2, S])
    stat = sb("stt", [P, 2, 3, 8])
    pt = sb("pt", [P, 2, S])
    on = sb("on", [P, S])
    oT = sb("oT", [P, HP, S])
    h = sb("h", [P, NJ, S])
    gl = sb("gl", [P, NJ, S])

    d_w = sem("d_lw")
    s_set = sem("s_set")
    (s_xs, s_v, s_vev, s_ab, s_sq, s_rot, s_g, s_ssq, s_r, s_ln, s_add, s_qkn) = (
        sem(x) for x in ("t_xs", "t_v", "t_vev", "t_ab", "t_sq", "t_rot", "t_g", "t_ssq", "t_r", "t_ln", "t_add", "t_qkn"))
    (s_S, s_m, s_sub, s_exp, s_rs, s_ri, s_pn, s_pt, s_ptev, s_o, s_oev, s_ot, s_otev, s_wo) = (
        sem(x) for x in ("t_S", "t_m", "t_sub", "t_exp", "t_rs", "t_ri", "t_pn", "t_pt", "t_ptev", "t_o", "t_oev",
                         "t_ot", "t_otev", "t_wo"))
    (s_x1, s_xs2, s_mean, s_xc, s_sq2, s_var, s_ge, s_rr, s_xn, s_w1, s_gl, s_h, s_w2, s_x2) = (
        sem(x) for x in ("t_x1", "t_xs2", "t_mean", "t_xc", "t_sq2", "t_var", "t_ge", "t_rr", "t_xn", "t_w1", "t_gl",
                         "t_h", "t_w2", "t_x2"))
    A, BB, SS, S0, S1, TT, O0, O1 = range(8)
    NV = 16
    clear()

    with nc.Block(no_gpsimd_drain=True) as block:
        @block.vector
        def _(dve):
            nc.vector.memset(xs[:], 0.0).then_inc(s_set, 1)
            nc.vector.memset(kn[:], 0.0).then_inc(s_set, 1)
            nc.vector.tensor_copy(maskb[:], con[:, C_MASK:C_MASK + 256]).then_inc(s_set, 1)
            nc.vector.tensor_copy(identb[:], ident).then_inc(s_set, 1)
            dve.wait_ge(s_set, 4)
    clear()

    with nc.Fori(0, DEPTH) as l:
        n_dma = 3 + NJ + 16 + 3 + 2 * NJ
        with nc.Block(no_gpsimd_drain=True) as block:
            @block.sync
            def _(sp):
                sp.dma_start(w[:], t["L0_ffn_Wqkv"][l]).then_inc(d_w, 16)
                sp.dma_start(wo[:], t["L0_ffn_Wo"][l].rearrange("(a p) n -> p a n", p=P)).then_inc(d_w, 16)
                sp.dma_start(w1[:], t["L0_ffn_W1"][l]).then_inc(d_w, 16)
                for j in range(NJ):
                    sp.dma_start(w2[0:JW[j], j, :], t["L0_ffn_W2"][l, j * P:j * P + JW[j], :]).then_inc(d_w, 16)

            @block.vector
            def _(dve):
                dve.wait_ge(d_w, 16 * n_dma)
                for i, (c, s) in enumerate(((C_QC, 0), (C_QS, 1), (C_KC, 2), (C_KS, 3))):
                    nc.vector.tensor_scalar(tab[:, i, :], con[:, c:c + S], vec[:, s:s + 1], None,
                                            ALU.mult).then_inc(s_set, 1)
                dve.wait_ge(s_set, 4)

            @block.scalar
            def _(act):
                for i, n in ((0, "L0_ffn_q_scale"), (2, "L0_ffn_k_scale")):
                    src = t[n].rearrange("l (d o) -> l d o", o=1)
                    for g in range(4):
                        own, other = (g % 2) * HALF, (1 - g % 2) * HALF
                        act.dma_start(vec[g * HALF:(g + 1) * HALF, i:i + 1], src[l, own:own + HALF]).then_inc(d_w, 16)
                        act.dma_start(vec[g * HALF:(g + 1) * HALF, i + 1:i + 2], src[l, other:other + HALF]).then_inc(d_w, 16)
                for i, n in ((V_G, "L0_ffn_ln_g"), (V_B, "L0_ffn_ln_b"), (V_B2, "L0_ffn_b2")):
                    act.dma_start(vec[:, i:i + 1], t[n].rearrange("l (d o) -> l d o", o=1)[l]).then_inc(d_w, 16)
                b1 = t["L0_ffn_b1"].rearrange("l (d o) -> l d o", o=1)
                for a in range(2):
                    for j in range(NJ):
                        c = V_B1 + a * NJ + j
                        o = a * DI + j * P
                        act.dma_start(vec[0:JW[j], c:c + 1], b1[l, o:o + JW[j]]).then_inc(d_w, 16)
                act.wait_ge(d_w, 16 * n_dma)
                src = w[:, 0:2 * INNER].rearrange("p (h t d) -> p h t d", t=2, d=HALF)
                dst = wsw[:].rearrange("p (h t d) -> p h t d", t=2, d=HALF)
                for a in range(2):
                    nc.scalar.copy(dst[:, :, a, :], src[:, :, 1 - a, :])
        clear()
        with nc.Fori(0, B) as b:
            with nc.Block(no_gpsimd_drain=True) as block:
                def win(ap, base, wd, n=WIN):
                    return ap[:, base + WIN * wd:base + WIN * wd + n]

                @block.tensor
                def _(pe):
                    pe.wait_ge(s_xs, 2)
                    for j in range(NV):
                        sh, tb, hf = j // 8, j // 2 % 4, j % 2
                        if j >= 5:
                            pe.wait_ge(s_vev, j - 4)
                        o = WIN + tb * P - WIN * sh
                        nc.tensor.matmul(ps[:, 3 + j % 5, :], xs[:, o:o + P],
                                         w[:, 2 * INNER + 512 * hf:2 * INNER + 512 * hf + 512],
                                         start=True, stop=True).then_inc(s_v, 1)

                    def project(i, k):
                        n = 2 * i + k
                        c = k * INNER + i * P
                        if n >= 1:
                            pe.wait_ge(s_rot, n)
                            pe.wait_ge(s_sq, n)
                        x = xs[:, WIN:]
                        nc.tensor.matmul(ps[:, A, :], w[:, c:c + P], x, start=True, stop=True)
                        nc.tensor.matmul(ps[:, BB, :], wsw[:, c:c + P], x, start=True, stop=True).then_inc(s_ab, 1)

                    def squares(i, k):
                        n = 2 * i + k
                        pe.wait_ge(s_sq, n + 1)
                        if n >= 1:
                            pe.wait_ge(s_g, n)
                        nc.tensor.matmul(ps[:, SS, :], con[:, C_PAIR:C_PAIR + P], sq[:, n % 2, :],
                                         start=True, stop=True).then_inc(s_ssq, 1)

                    def scores(i):
                        if i == 0:
                            pe.wait_ge(s_vev, NV)
                        if i >= 1:
                            pe.wait_ge(s_sub, i)
                        for e in range(2):
                            nc.tensor.matmul(ps[:, S0 + e, 0:256], identb[:], maskb[:], start=True, stop=False,
                                             skip_group_check=True)
                        pe.wait_ge(s_qkn, 2 * i + 2)
                        for e in range(2):
                            q = qn[e * DH:(e + 1) * DH, i % 2, :]
                            k = kn[e * DH:(e + 1) * DH, i % 2, :]
                            for wd in range(S // WIN):
                                tb, whi, wlo = wd // 4, wd // 2 % 2, wd % 2
                                strip = (tb % 2 * 2 + wlo) * WIN
                                col = (tb // 2 * 2 + whi) * 2 * WIN
                                last = nc.tensor.matmul(
                                    ps[strip:strip + WIN, S0 + e, col:col + 2 * WIN], win(q, 0, wd),
                                    win(k, 0, wd, 2 * WIN), start=False, stop=True, skip_group_check=True,
                                    tile_position=(e * DH, strip))
                        last.then_inc(s_S, 1)

                    def turn_probs(i):
                        pe.wait_ge(s_pn, i + 1)
                        if i >= 1:
                            pe.wait_ge(s_otev, i)
                        for m in range(4):
                            last = nc.tensor.transpose(ps[:, TT, m * P:(m + 1) * P], pr[:, i % 2, m * P:(m + 1) * P],
                                                       ident)
                        last.then_inc(s_pt, 1)

                    def values(i):
                        pe.wait_ge(s_ptev, i + 1)
                        if i >= 1:
                            pe.wait_ge(s_oev, i)
                        for whi in range(2):
                            for tb in range(TB):
                                for wlo in range(2):
                                    for e in range(2):
                                        strip = (tb % 2 * 2 + wlo) * WIN
                                        c = (e * 2 + tb // 2) * P + strip
                                        o = (tb // 2) * P + e * DH
                                        hh = 2 * i + e
                                        last = nc.tensor.matmul(
                                            ps[strip:strip + WIN, O0 + whi, o:o + DH],
                                            pt[whi * DH:(whi + 1) * DH, i % 2, c:c + WIN],
                                            v[whi * DH:(whi + 1) * DH, 1 - wlo, tb, hh * DH:(hh + 1) * DH],
                                            start=True, stop=True, skip_group_check=True,
                                            tile_position=(whi * DH, strip))
                        last.then_inc(s_o, 1)

                    def turn_out(i):
                        pe.wait_ge(s_oev, i + 1)
                        for m in range(4):
                            last = nc.tensor.transpose(ps[:, TT, m * P:(m + 1) * P], on[:, m * P:(m + 1) * P], ident)
                        last.then_inc(s_ot, 1)

                    for i in range(HP + 3):
                        if i >= 3:
                            turn_out(i - 3)
                        if i < HP:
                            project(i, 0)
                        if 1 <= i <= HP:
                            scores(i - 1)
                        if i < HP:
                            squares(i, 0)
                            project(i, 1)
                        if 2 <= i <= HP + 1:
                            turn_probs(i - 2)
                        if i < HP:
                            squares(i, 1)
                        if 2 <= i <= HP + 1:
                            values(i - 2)
                    pe.wait_ge(s_otev, HP)
                    for i in range(HP):
                        last = nc.tensor.matmul(ps[:, A, :], wo[:, i, :], oT[:, i, :], start=(i == 0), stop=(i == HP - 1))
                    last.then_inc(s_wo, 1)
                    pe.wait_ge(s_xs2, 2)
                    nc.tensor.matmul(ps[:, SS, :], con[:, C_MEAN:C_MEAN + P], xs[:, WIN:], start=True,
                                     stop=True).then_inc(s_mean, 1)
                    pe.wait_ge(s_sq2, 1)
                    nc.tensor.matmul(ps[:, BB, :], con[:, C_MEAN:C_MEAN + P], sq[:, 0, :], start=True,
                                     stop=True).then_inc(s_var, 1)
                    pe.wait_ge(s_xn, 2)
                    pe.wait_ge(s_x1, 1)
                    up = (S0, S1, O0), (O1, TT, A)
                    for j in range(NJ):
                        for a in (1, 0):
                            c = a * DI + j * P
                            nc.tensor.matmul(ps[0:JW[j], up[a][j], :], w1[:, c:c + JW[j]], rb[:, 0, :],
                                             start=True, stop=True).then_inc(s_w1, 1)
                    for j in range(NJ):
                        pe.wait_ge(s_h, j + 1)
                        last = nc.tensor.matmul(ps[:, BB, :], w2[0:JW[j], j, :], h[0:JW[j], j, :], start=(j == 0),
                                                stop=(j == NJ - 1))
                    last.then_inc(s_w2, 1)

                @block.scalar
                def _(act):
                    nc.scalar.preload_act_table_set("natural_log_exp_and_others")
                    for j in range(NV):
                        sh, tb, hf = j // 8, j // 2 % 4, j % 2
                        act.wait_ge(s_v, j + 1)
                        nc.scalar.copy(v[:, sh, tb, hf * 512:(hf + 1) * 512], ps[:, 3 + j % 5, :]).then_inc(s_vev, 1)

                    def square(i, k):
                        n = 2 * i + k
                        act.wait_ge(s_ab, n + 1)
                        if n >= 2:
                            act.wait_ge(s_ssq, n - 1)
                        nc.scalar.activation(sq[:, n % 2, :], ps[:, A, :], ACT.Square).then_inc(s_sq, 1)

                    def inverse_norm(i, k):
                        n = 2 * i + k
                        act.wait_ge(s_g, n + 1)
                        nc.scalar.activation(r1[:, n % 2, :], r1[:, n % 2, :], ACT.Ln, scale=RN * RN).then_inc(s_ln, 1)
                        act.wait_ge(s_ln, n + 1)
                        nc.scalar.activation(r1[:, n % 2, :], r1[:, n % 2, :], ACT.Exp, scale=-0.5).then_inc(s_r, 1)

                    def exponentials(i):
                        act.wait_ge(s_sub, i + 1)
                        nc.scalar.activation(pr[:, i % 2, :], pr[:, i % 2, :], ACT.Exp).then_inc(s_exp, 1)

                    for i in range(HP + 3):
                        if i >= 3:
                            act.wait_ge(s_ot, i - 2)
                            nc.scalar.copy(oT_view(oT, i - 3),
                                           ps[:, TT, :].rearrange("p (wh t2 t1 s) -> p wh t2 t1 s", wh=2, t2=2, t1=2)) \
                               .then_inc(s_otev, 1)
                        if i < HP:
                            square(i, 0)
                        if 1 <= i <= HP:
                            exponentials(i - 1)
                        if i < HP:
                            inverse_norm(i, 0)
                            square(i, 1)
                        if 2 <= i <= HP + 1:
                            act.wait_ge(s_pt, i - 1)
                            nc.scalar.copy(pt[:, i % 2, :], ps[:, TT, :]).then_inc(s_ptev, 1)
                        if i < HP:
                            inverse_norm(i, 1)
                        if 2 <= i <= HP + 1:
                            act.wait_ge(s_o, i - 1)
                            if i >= 3:
                                act.wait_ge(s_ot, i - 2)
                            nc.scalar.copy(on[:].rearrange("p (w c) -> p w c", w=2), ps[:, O0:O1 + 1, 0:256]) \
                               .then_inc(s_oev, 1)
                    act.wait_ge(s_xc, 1)
                    nc.scalar.activation(sq[:, 0, :], ra[:, 0, :], ACT.Square).then_inc(s_sq2, 1)
                    act.wait_ge(s_ge, 1)
                    nc.scalar.activation(r1[:, 0, :], r1[:, 0, :], ACT.Ln).then_inc(s_ge, 1)
                    act.wait_ge(s_ge, 2)
                    nc.scalar.activation(r1[:, 0, :], r1[:, 0, :], ACT.Exp, scale=-0.5).then_inc(s_rr, 1)
                    for j in range(NJ):
                        act.wait_ge(s_w1, 2 * j + 1)
                        m = JW[j]
                        nc.scalar.activation(gl[0:m, j, :], ps[0:m, (O1, TT, A)[j], :], ACT.Gelu,
                                             bias=vec[0:m, V_B1 + NJ + j:V_B1 + NJ + j + 1]).then_inc(s_gl, 1)

                @block.gpsimd
                def _(pool):
                    def rotate(i, k):
                        n = 2 * i + k
                        pool.wait_ge(s_rot, n + 1)
                        nc.gpsimd.tensor_tensor(ra[:, n % 2, :], ra[:, n % 2, :], rb[:, n % 2, :], ALU.add).then_inc(s_add, 1)
                        pool.wait_ge(s_add, n + 1)
                        pool.wait_ge(s_r, n + 1)
                        if i >= 2:
                            pool.wait_ge(s_S, i - 1)
                        dst = kn[:, i % 2, WIN:] if k else qn[:, i % 2, :]
                        nc.gpsimd.tensor_tensor(dst, ra[:, n % 2, :], r1[:, n % 2, :], ALU.mult).then_inc(s_qkn, 1)

                    for i in range(HP + 1):
                        if i < HP:
                            rotate(i, 0)
                        if i >= 1:
                            pool.wait_ge(s_ri, i)
                            p3 = pr[:, (i - 1) % 2, :].rearrange("p (g k) -> p g k", g=8)
                            nc.gpsimd.tensor_tensor(p3, p3, stat[:, (i - 1) % 2, 2, :].unsqueeze(2)
                                                    .broadcast_to([P, 8, 64]), ALU.mult).then_inc(s_pn, 1)
                        if i < HP:
                            rotate(i, 1)

                @block.vector
                def _(dve):
                    nc.vector.tensor_copy(xs[0:64, WIN:], xT[0:64, b, :]).then_inc(s_xs, 1)
                    nc.vector.tensor_copy(xs[64:128, WIN + 1:], xT[64:128, b, 0:S - 1]).then_inc(s_xs, 1)

                    def rotary(i, k):
                        n = 2 * i + k
                        dve.wait_ge(s_ab, n + 1)
                        if n >= 2:
                            dve.wait_ge(s_qkn, n - 1)
                        nc.vector.tensor_tensor(rb[:, n % 2, :], ps[:, BB, :], tab[:, 2 * k + 1, :], ALU.mult)
                        dve.wait_ge(s_sq, n + 1)
                        nc.vector.tensor_tensor(ra[:, n % 2, :], ps[:, A, :], tab[:, 2 * k, :],
                                                ALU.mult).then_inc(s_rot, 1)

                    def guard(i, k):
                        n = 2 * i + k
                        dve.wait_ge(s_ssq, n + 1)
                        if n >= 2:
                            dve.wait_ge(s_qkn, n - 1)
                        nc.vector.tensor_scalar(r1[:, n % 2, :], ps[:, SS, :], 1e-24, None, ALU.max).then_inc(s_g, 1)

                    def subtract_max(i):
                        dve.wait_ge(s_S, i + 1)
                        s4 = ps[:, S0:S1 + 1, 0:256].rearrange("p e (g k) -> p e g k", g=4)
                        if i >= 2:
                            dve.wait_ge(s_pt, i - 1)
                        nc.vector.tensor_reduce(stat[:, i % 2, 0, :].rearrange("p (e g) -> p e g", e=2), s4, AX_X,
                                                ALU.max).then_inc(s_m, 1)
                        dve.wait_ge(s_m, i + 1)
                        nc.vector.tensor_tensor(pr[:, i % 2, :].rearrange("p (e g k) -> p e g k", e=2, g=4), s4,
                                                stat[:, i % 2, 0, :].rearrange("p (e g) -> p e g", e=2).unsqueeze(3)
                                                .broadcast_to([P, 2, 4, 64]), ALU.subtract).then_inc(s_sub, 1)

                    def row_sums(i):
                        dve.wait_ge(s_exp, i + 1)
                        nc.vector.tensor_reduce(stat[:, i % 2, 1, :], pr[:, i % 2, :].rearrange("p (g k) -> p g k", g=8),
                                                AX_X, ALU.add).then_inc(s_rs, 1)
                        dve.wait_ge(s_rs, i + 1)
                        nc.vector.reciprocal(stat[:, i % 2, 2, :], stat[:, i % 2, 1, :]).then_inc(s_ri, 1)

                    for i in range(HP + 1):
                        if i < HP:
                            rotary(i, 0)
                        if i >= 1:
                            subtract_max(i - 1)
                        if i < HP:
                            guard(i, 0)
                            rotary(i, 1)
                        if i >= 1:
                            row_sums(i - 1)
                        if i < HP:
                            guard(i, 1)
                    dve.wait_ge(s_wo, 1)
                    nc.vector.tensor_tensor(xT[:, b, :], ps[:, A, :], xT[:, b, :], ALU.add).then_inc(s_x1, 1)
                    dve.wait_ge(s_x1, 1)
                    nc.vector.tensor_copy(xs[0:64, WIN:], xT[0:64, b, :]).then_inc(s_xs2, 1)
                    nc.vector.tensor_copy(xs[64:128, WIN + 1:], xT[64:128, b, 0:S - 1]).then_inc(s_xs2, 1)
                    dve.wait_ge(s_mean, 1)
                    nc.vector.tensor_tensor(ra[:, 0, :], xs[:, WIN:], ps[:, SS, :], ALU.subtract).then_inc(s_xc, 1)
                    dve.wait_ge(s_var, 1)
                    nc.vector.tensor_scalar(r1[:, 0, :], ps[:, BB, :], EPS, None, ALU.add).then_inc(s_ge, 1)
                    dve.wait_ge(s_rr, 1)
                    nc.vector.tensor_tensor(rb[:, 0, :], ra[:, 0, :], r1[:, 0, :], ALU.mult).then_inc(s_xn, 1)
                    dve.wait_ge(s_xn, 1)
                    nc.vector.tensor_scalar(rb[:, 0, :], rb[:, 0, :], vec[:, V_G:V_G + 1], vec[:, V_B:V_B + 1],
                                            ALU.mult, ALU.add).then_inc(s_xn, 1)
                    for j in range(NJ):
                        m = JW[j]
                        dve.wait_ge(s_w1, 2 * j + 2)
                        dve.wait_ge(s_gl, j + 1)
                        nc.vector.scalar_tensor_tensor(out=h[0:m, j, :], in0=ps[0:m, (S0, S1, O0)[j], :],
                                                       scalar=vec[0:m, V_B1 + j:V_B1 + j + 1], in1=gl[0:m, j, :],
                                                       op0=ALU.add, op1=ALU.mult).then_inc(s_h, 1)
                    dve.wait_ge(s_w2, 1)
                    nc.vector.scalar_tensor_tensor(out=xT[:, b, :], in0=ps[:, BB, :], scalar=vec[:, V_B2:V_B2 + 1],
                                                   in1=xT[:, b, :], op0=ALU.add, op1=ALU.add).then_inc(s_x2, 1)
                    dve.wait_ge(s_x2, 1)
            clear()


def oT_view(oT, i):
    return oT[:, i, :].rearrange("p (t2 t1 wh s) -> p wh t2 t1 s", t2=2, t1=2, wh=2)


_INS = ['L0_attn_hidden_states', 'L0_attn_position_embeddings', 'L0_attn_Wq', 'L0_attn_Wk', 'L0_attn_Wv',
        'L0_attn_Wpost', 'L0_attn_Wrel', 'L0_attn_per_dim_scale', 'L0_ffn_Wqkv', 'L0_ffn_q_scale',
        'L0_ffn_k_scale', 'L0_ffn_Wo', 'L0_ffn_ln_g', 'L0_ffn_ln_b', 'L0_ffn_W1', 'L0_ffn_b1', 'L0_ffn_W2',
        'L0_ffn_b2']


def kernel(**inputs):
    import concourse.bacc as bacc
    from concourse.bass_utils import run_bass_kernel_spmd

    nc = bacc.Bacc("TRN2", target_bir_lowering=False, num_devices=1)
    arrays, args = {}, {}
    for name in _INS + ["consts"]:
        a = np.ascontiguousarray(inputs[name]) if name != "consts" else constants()
        arrays[f"in_{name}"] = a
        args[name] = nc.dram_tensor(f"in_{name}", a.shape, mybir.dt.from_np(a.dtype), kind="ExternalInput").ap()
    out = nc.dram_tensor("out_0", (B, S, D), F32, kind="ExternalOutput").ap()
    build(nc, args, out)
    r = run_bass_kernel_spmd(nc, [arrays], core_ids=[0])
    return r.results[0]["out_0"]
```

```python
import math
from contextlib import ExitStack

import numpy as np

import concourse.bass as bass
from concourse import mybir

ALU = mybir.AluOpType
ACT = mybir.ActivationFunctionType
F32 = mybir.dt.float32
BF16 = mybir.dt.bfloat16
F32R = mybir.dt.float32r
AX_X = mybir.AxisListType.X

P = 128
B, S, D = 8, 512, 128
TB = S // P
EPS = 1e-5

CH, CCH, CD = 8, 12, 16
CTX = 2 * CCH
NPOS = CTX + 1
NB = -(-S // CCH)
SP = NB * CCH
NTILE = -(-B * NB // P)
TW = P * CCH
SOFTCAP = 50.0
Q_SCALE = CD ** -0.5 / math.log(2)
K_SCALE = math.log(1.0 + math.e) / math.log(2)

DEPTH, HEADS, DH, WIN = 6, 16, 64, 32
INNER = HEADS * DH
HP = HEADS // 2
HALF = DH // 2
DI = int(D * 4 * 2 / 3)
NJ = -(-DI // P)
JW = [min(P, DI - P * j) for j in range(NJ)]
NEG = -1e30
LN_EXP = "natural_log_exp_and_others"
RN = 256.0

C_ID, C_MASK, C_PAIR, C_MEAN, C_HM, C_PM = 0, 128, 384, 512, 640, 648
C_END = C_PM + NTILE


def constants():
    c = np.zeros((P, C_END), np.float32)
    c[:, C_ID:C_ID + P] = np.eye(P)
    i = np.arange(P) % WIN
    j = np.arange(2 * WIN)
    ok = (j[None] >= i[:, None]) & (j[None] <= i[:, None] + WIN)
    mask = np.tile(np.where(ok, 0.0, NEG), (1, 4)).astype(np.float32)
    mask[0:WIN, 0:WIN] = NEG
    c[:, C_MASK:C_MASK + 256] = mask
    p = np.arange(P)
    c[:, C_PAIR:C_PAIR + P] = p[:, None] // DH == p[None] // DH
    c[:, C_MEAN:C_MEAN + P] = 1.0 / D
    c[:, C_HM:C_HM + CH] = p[:, None] // CD == np.arange(CH)[None]
    for n in range(NTILE):
        c[:, C_PM + n] = (n * P + p) % NB != 0
    return c


def rotary_tables():
    f = np.float32
    half = np.arange(0, DH, 2, dtype=f)
    inv_freq = (f(1.0) / f(10000.0) ** (half / f(DH))).astype(f)
    t = np.arange(S, dtype=f)
    freqs = t[:, None] * inv_freq[None]
    base = (half + f(0.4 * DH)) / f(1.4 * DH)
    power = ((t - S // 2) / f(WIN // 2)).astype(f)
    scale = base[None] ** power[:, None]
    cos, sin = np.cos(freqs), np.sin(freqs)
    sign = np.where(np.arange(P) % DH < HALF, -1.0, 1.0).astype(f)[:, None]
    four = lambda a: np.tile(a.T, (4, 1)).astype(f)
    tables = (8 * RN * four(cos * scale), 8 * RN * four(sin * scale) * sign,
              RN * four(cos / scale), RN * four(sin / scale) * sign)
    return np.stack(tables, axis=1).astype(f)


def build(nc, t, out):
    with ExitStack() as top:
        def sb(name, shape, dt=F32, ctx=top):
            return ctx.enter_context(nc.sbuf_tensor(name, shape, dt))

        sems = []

        def sem(name, keep=False):
            s = top.enter_context(nc.semaphore(name))
            if not keep:
                sems.append(s.num)
            return s

        ps = top.enter_context(nc.psum_tensor("ps", [P, 8, 512], F32))
        con = sb("con", [P, C_END])
        xT = sb("xT", [P, B + 1, S])
        sT = nc.dram_tensor("sT", (P, NTILE * TW), F32, kind="Internal").ap()
        ident = con[:, C_ID:C_ID + P]

        d_raw = sem("d_raw", keep=True)
        d_in, d_out = sem("d_in"), sem("d_out")

        def clear():
            nc.sync.sem_clear(range(min(sems), max(sems) + 1))
            nc.all_engine_barrier()

        clear()

        conf = ExitStack()
        cx = sb("cx", [P, CCH + NTILE * TW], ctx=conf)
        s_zero, s_stat, s_var, s_rs, s_xn, s_tr, s_xt = (
            sem("s_zero"), sem("s_stat"), sem("s_var"), sem("s_rs"), sem("s_xn"), sem("s_tr"), sem("s_xt"))
        with ExitStack() as ctx:
            xnat = sb("xnat", [P, B, TB, D], ctx=ctx)
            stat = sb("stat", [P, TB, 6], ctx=ctx)
            mv = sb("mv", [P, TB, 2], ctx=ctx)
            lnv = sb("lnv", [P, TB], ctx=ctx)
            rstd = sb("rstd", [P, TB], ctx=ctx)
            xn = sb("xn", [P, TB, D], ctx=ctx)
            with nc.Block(no_gpsimd_drain=True) as block:
                @block.sync
                def _(sp):
                    sp.dma_start(con[:], t["consts"]).then_inc(d_in, 16)
                    sp.dma_start(xnat[:].rearrange("p b t d -> p (b t) d"),
                                 t["L0_attn_hidden_states"].rearrange("b (t p) d -> p (b t) d", p=P)).then_inc(d_in, 16)
                    sp.wait_ge(d_in, 32)

                @block.vector
                def _(dve):
                    nc.vector.memset(cx[:], 0.0).then_inc(s_zero, 1)
                    dve.wait_ge(s_zero, 1)
            clear()
            with nc.Fori(0, B) as b:
                with nc.Block(no_gpsimd_drain=True) as block:
                    @block.vector
                    def _(dve):
                        for k in range(TB):
                            nc.vector.bn_stats(stat[:, k, :], xnat[:, b, k, :]).then_inc(s_stat, 1)
                        dve.wait_ge(s_stat, TB)
                        for k in range(TB):
                            nc.vector.bn_aggr(mv[:, k, :], stat[:, k, :]).then_inc(s_stat, 1)
                        dve.wait_ge(s_stat, 2 * TB)
                        nc.vector.tensor_scalar(lnv[:], mv[:, :, 1], EPS, None, ALU.add).then_inc(s_var, 1)
                        dve.wait_ge(s_rs, 1)
                        for k in range(TB):
                            nc.vector.tensor_scalar(xn[:, k, :], xnat[:, b, k, :], mv[:, k, 0:1],
                                                    rstd[:, k:k + 1], ALU.subtract, ALU.mult).then_inc(s_xn, 1)

                    @block.scalar
                    def _(act):
                        act.wait_ge(s_var, 1)
                        nc.scalar.activation(lnv[:], lnv[:], ACT.Ln).then_inc(s_var, 1)
                        act.wait_ge(s_var, 2)
                        nc.scalar.activation(rstd[:], lnv[:], ACT.Exp, scale=-0.5).then_inc(s_rs, 1)
                        act.wait_ge(s_tr, 1)
                        nc.scalar.copy(xT[:, b, :], ps[:, 0, :]).then_inc(s_xt, 1)
                        act.wait_ge(s_xt, 1)
                        nc.scalar.copy(cx[:, bass.ds(b * SP + CCH, S)], xT[:, b, :])

                    @block.tensor
                    def _(pe):
                        for k in range(TB):
                            pe.wait_ge(s_xn, k + 1)
                            last = nc.tensor.transpose(ps[:, 0, k * P:(k + 1) * P], xn[:, k, :], ident)
                        last.then_inc(s_tr, 1)
                clear()

        with conf:
            chunked_attention(nc, t, conf, sb, sem, clear, con, ident, ps, cx, sT)

        with ExitStack() as ctx:
            transformer(nc, t, ctx, sb, sem, clear, con, ident, ps, xT, d_raw)

        s_z, s_y, s_t4, s_o = sem("s_z"), sem("s_y"), sem("s_t4"), sem("s_o")
        with ExitStack() as ctx:
            d_s = sem("d_s")
            srow = sb("srow", [P, S], ctx=ctx)
            z = sb("z", [P, S], ctx=ctx)
            y = sb("y", [P, S], ctx=ctx)
            xrow = sb("xrow", [P, TB, D], ctx=ctx)
            orow = sb("orow", [P, TB, D], ctx=ctx)
            clear()
            with nc.Fori(0, B) as b:
                with nc.Block(no_gpsimd_drain=True) as block:
                    @block.sync
                    def _(sp):
                        sp.dma_start(xrow[:], t["L0_attn_hidden_states"].rearrange(
                            "b (t p) d -> p b t d", p=P)[:, b]).then_inc(d_in, 16)
                        sp.dma_start(srow[:], sT[:, bass.ds(b * SP, S)]).then_inc(d_s, 16)
                        sp.wait_ge(s_o, 1)
                        sp.dma_start(out.rearrange("b (t p) d -> p b t d", p=P)[:, b], orow[:]).then_inc(d_out, 16)
                        sp.wait_ge(d_out, 16)

                    @block.scalar
                    def _(act):
                        nc.scalar.activation(z[:], xT[:, b, :], ACT.Silu).then_inc(s_z, 1)

                    @block.vector
                    def _(dve):
                        dve.wait_ge(s_z, 1)
                        dve.wait_ge(d_s, 16)
                        nc.vector.tensor_tensor(y[:], srow[:], z[:], ALU.mult).then_inc(s_y, 1)
                        dve.wait_ge(s_t4, 1)
                        dve.wait_ge(d_in, 16)
                        nc.vector.tensor_tensor(orow[:], ps[:, 0, :].rearrange("p (t d) -> p t d", t=TB),
                                                xrow[:], ALU.add).then_inc(s_o, 1)

                    @block.tensor
                    def _(pe):
                        pe.wait_ge(s_y, 1)
                        for k in range(TB):
                            last = nc.tensor.transpose(ps[:, 0, k * P:(k + 1) * P], y[:, k * P:(k + 1) * P], ident)
                        last.then_inc(s_t4, 1)
                clear()


def chunked_attention(nc, t, ctx0, sb, sem, clear, con, ident, ps, cx, sT):
    d_st = sem("d_st")
    d_w, s_sp, s_ws, s_wt, s_we, s_re = (
        sem("d_w"), sem("s_sp"), sem("s_ws"), sem("s_wt"), sem("s_we"), sem("s_re"))
    with ExitStack() as ctx:
        names = ["L0_attn_Wq", "L0_attn_Wk", "L0_attn_Wv", "L0_attn_Wpost", "L0_attn_Wrel"]
        wnat = sb("wnat", [P, 5, P], ctx=ctx)
        pos = sb("pos", [NPOS, P], ctx=ctx)
        pds = sb("pds", [P, 6], ctx=ctx)
        wqs = sb("wqs", [P, P], ctx=ctx)
        wrelT = sb("wrelT", [P, P], ctx=ctx)
        posT = sb("posT", [P, NPOS], ctx=ctx)
        relT = sb("relT", [P, NPOS], ctx=ctx)
        relE = sb("relE", [P, CH, NPOS], ctx=ctx)
        wqkv = sb("cwqkv", [P, 3 * P], ctx=ctx)
        wqr = sb("wqr", [P, CH * NPOS], ctx=ctx)
        wpostT = sb("wpostT", [P, P], ctx=ctx)
        clear()
        with nc.Block(no_gpsimd_drain=True) as block:
            @block.sync
            def _(sp):
                for i, n in enumerate(names):
                    sp.dma_start(wnat[:, i, :], t[n]).then_inc(d_w, 16)
                sp.dma_start(pos[:], t["L0_attn_position_embeddings"]).then_inc(d_w, 16)
                for h in range(CH):
                    sp.dma_start(pds[h * CD:(h + 1) * CD, 0:1],
                                 t["L0_attn_per_dim_scale"].rearrange("(d o) -> d o", o=1)).then_inc(d_w, 16)

            @block.vector
            def _(dve):
                dve.wait_ge(d_w, 16 * (6 + CH))
                nc.vector.scalar_tensor_tensor(out=pds[:, 1:2], in0=pds[:, 0:1], scalar=-1.0, in1=pds[:, 0:1],
                                               op0=ALU.mult, op1=ALU.min).then_inc(s_sp, 1)
                dve.wait_ge(s_sp, 2)
                nc.vector.tensor_scalar(pds[:, 3:4], pds[:, 2:3], 1.0, None, ALU.add).then_inc(s_sp, 1)
                dve.wait_ge(s_sp, 4)
                nc.vector.scalar_tensor_tensor(out=pds[:, 5:6], in0=pds[:, 0:1], scalar=0.0, in1=pds[:, 4:5],
                                               op0=ALU.max, op1=ALU.add).then_inc(s_sp, 1)
                dve.wait_ge(s_sp, 5)
                nc.vector.tensor_scalar(wqs[:], wnat[:, 0, :], pds[:, 5:6], Q_SCALE,
                                        ALU.mult, ALU.mult).then_inc(s_ws, 1)
                dve.wait_ge(s_wt, 7)
                nc.vector.tensor_copy(relT[:], ps[:, 6, 0:NPOS]).then_inc(s_re, 1)
                dve.wait_ge(s_re, 1)
                nc.vector.tensor_tensor(relE[:], relT[:].unsqueeze(1).broadcast_to([P, CH, NPOS]),
                                        con[:, C_HM:C_HM + CH].unsqueeze(2).broadcast_to([P, CH, NPOS]),
                                        ALU.mult).then_inc(s_re, 1)
                dve.wait_ge(s_wt, 8)
                nc.vector.tensor_copy(wqr[:], ps[:, 7, 0:CH * NPOS]).then_inc(s_re, 1)

            @block.scalar
            def _(act):
                act.wait_ge(s_sp, 1)
                nc.scalar.activation(pds[:, 2:3], pds[:, 1:2], ACT.Exp).then_inc(s_sp, 1)
                act.wait_ge(s_sp, 3)
                nc.scalar.activation(pds[:, 4:5], pds[:, 3:4], ACT.Ln).then_inc(s_sp, 1)
                act.wait_ge(s_wt, 6)
                nc.scalar.copy(wqkv[:, 0:P], ps[:, 0, 0:P]).then_inc(s_we, 1)
                nc.scalar.mul(wqkv[:, P:2 * P], ps[:, 1, 0:P], K_SCALE).then_inc(s_we, 1)
                nc.scalar.copy(wqkv[:, 2 * P:], ps[:, 2, 0:P]).then_inc(s_we, 1)
                nc.scalar.copy(wpostT[:], ps[:, 3, 0:P]).then_inc(s_we, 1)
                nc.scalar.copy(wrelT[:], ps[:, 4, 0:P]).then_inc(s_we, 1)
                nc.scalar.copy(posT[:], ps[:, 5, 0:NPOS]).then_inc(s_we, 1)

            @block.tensor
            def _(pe):
                pe.wait_ge(s_ws, 1)
                nc.tensor.transpose(ps[:, 0, 0:P], wqs[:], ident).then_inc(s_wt, 1)
                for i in range(1, 5):
                    nc.tensor.transpose(ps[:, i, 0:P], wnat[:, i, :], ident).then_inc(s_wt, 1)
                nc.tensor.transpose(ps[:, 5, 0:NPOS], pos[:], ident[0:NPOS, 0:NPOS]).then_inc(s_wt, 1)
                pe.wait_ge(s_we, 6)
                nc.tensor.matmul(ps[:, 6, 0:NPOS], wrelT[:], posT[:], start=True, stop=True).then_inc(s_wt, 1)
                pe.wait_ge(s_re, 2)
                nc.tensor.matmul(ps[:, 7, 0:CH * NPOS], wqs[:], relE[:].rearrange("p h r -> p (h r)"),
                                 start=True, stop=True).then_inc(s_wt, 1)
        clear()

        ct = sb("ct", [P, CCH + TW], ctx=ctx)
        pm = sb("pm", [P, 1], ctx=ctx)
        qb = sb("qb", [P, CCH, P], ctx=ctx)
        kv = sb("kv", [P, CTX, 2, P], ctx=ctx)
        rel = sb("rel", [P, CH, CCH * NPOS], ctx=ctx)
        sc = sb("sc", [P, CH, CCH, CTX], ctx=ctx)
        NPR = 4
        prod = sb("prod", [P, NPR, CH * CTX * CD], ctx=ctx)
        sm = sb("sm", [P, CH * CCH], ctx=ctx)
        ri = sb("ri", [P, CH * CCH], ctx=ctx)
        ob = sb("ob", [P, CCH, P], ctx=ctx)
        obT = sb("obT", [P, CCH, P], ctx=ctx)
        so = sb("so", [P, P, CCH], ctx=ctx)
        s_ct, s_pj, s_ev, s_ed, s_mul, s_red, s_sc, s_sm, s_ot, s_oe, s_wp, s_so = (
            sem("s_ct"), sem("s_pj"), sem("s_ev"), sem("s_ed"), sem("s_mul"), sem("s_red"), sem("s_sc"),
            sem("s_sm"), sem("s_ot"), sem("s_oe"), sem("s_wp"), sem("s_so"))
        s_mulp = sem("s_mulp")

        def key_product(eng, c):
            return eng.tensor_tensor(
                prod[:, c % NPR, :].rearrange("p (h k d) -> p h k d", h=CH, k=CTX),
                qb[:, c, :].rearrange("p (h d) -> p h d", h=CH).unsqueeze(2).broadcast_to([P, CH, CTX, CD]),
                kv[:, :, 0, :].rearrange("p k (h d) -> p h k d", h=CH), ALU.mult)

        def value_product(eng, c):
            return eng.tensor_tensor(
                prod[:, c % NPR, :].rearrange("p (h d k) -> p h d k", h=CH, d=CD),
                sc[:, :, c, :].unsqueeze(2).broadcast_to([P, CH, CD, CTX]),
                kv[:, :, 1, :].rearrange("p k (h d) -> p h d k", h=CH), ALU.mult)

        def on_pool(c):
            return c % 2 == 1

        with nc.Fori(0, NTILE) as n:
            with nc.Block(no_gpsimd_drain=True) as block:
                @block.scalar
                def _(act):
                    nc.scalar.copy(ct[:], cx[:, bass.ds(n * TW, CCH + TW)]).then_inc(s_ct, 1)
                    for c in range(CCH):
                        act.wait_ge(s_pj, 3 * c + 1)
                        nc.scalar.copy(qb[:, c, :], ps[:, 3 * c % 6, 0:P])
                        nc.scalar.copy(kv[:, CCH + c, :, :].rearrange("p a d -> p (a d)"),
                                       ps[:, 3 * c % 6, P:3 * P]).then_inc(s_ev, 1)
                    scores = sc[:].rearrange("p h c k -> p (h c k)")
                    act.wait_ge(s_sc, 1)
                    nc.scalar.activation(scores, scores, ACT.Tanh, scale=1.0 / SOFTCAP).then_inc(s_sc, 1)
                    act.wait_ge(s_sc, 2)
                    nc.scalar.activation(scores, scores, ACT.Exp, scale=SOFTCAP).then_inc(s_sc, 1)
                    for g in range(3):
                        act.wait_ge(s_ot, g + 1)
                        nc.scalar.copy(obT[:, 4 * g:4 * g + 4, :], ps[:, g, :].rearrange("p (c m) -> p c m", c=4)) \
                           .then_inc(s_oe, 1)
                    for g in range(3):
                        act.wait_ge(s_wp, g + 1)
                        nc.scalar.copy(so[:].rearrange("p m c -> p c m")[:, 4 * g:4 * g + 4, :],
                                       ps[:, 3 + g, :].rearrange("p (c m) -> p c m", c=4)).then_inc(s_so, 1)
                    act.wait_ge(s_so, 3)
                    act.dma_start(sT[:, bass.ds(n * TW, TW)], so[:].rearrange("p m c -> p (m c)")).then_inc(d_st, 16)
                    act.wait_ge(d_st, 16)

                @block.tensor
                def _(pe):
                    pe.wait_ge(s_ct, 1)
                    for c in range(CCH):
                        own = ct[:, CCH + c:CCH + c + (P - 1) * CCH + 1:CCH]
                        prev = ct[:, c:c + (P - 1) * CCH + 1:CCH]
                        if c >= 2:
                            pe.wait_ge(s_ev, c - 1)
                            pe.wait_ge(s_ed, 2 * (c - 1))
                        k = 3 * c % 6
                        nc.tensor.matmul(ps[:, k, 0:3 * P], own, wqkv[:], start=True, stop=True).then_inc(s_pj, 1)
                        nc.tensor.matmul(ps[:, k + 1, 0:CH * NPOS], own, wqr[:], start=True, stop=True).then_inc(s_pj, 1)
                        nc.tensor.matmul(ps[:, k + 2, 0:2 * P], prev, wqkv[:, P:], start=True, stop=True).then_inc(s_pj, 1)
                    pe.wait_ge(s_ev, CCH)
                    pe.wait_ge(s_ed, 2 * CCH)
                    for g in range(3):
                        pe.wait_ge(s_red, CCH + 4 * g + 4)
                        for c in range(4):
                            last = nc.tensor.transpose(ps[:, g, c * P:(c + 1) * P], ob[:, 4 * g + c, :], ident)
                        last.then_inc(s_ot, 1)
                    for g in range(3):
                        pe.wait_ge(s_oe, g + 1)
                        nc.tensor.matmul(ps[:, 3 + g, :], wpostT[:],
                                         obT[:, 4 * g:4 * g + 4, :].rearrange("p c m -> p (c m)"),
                                         start=True, stop=True).then_inc(s_wp, 1)

                @block.gpsimd
                def _(pool):
                    pool.wait_ge(s_ev, CCH)
                    pool.wait_ge(s_ed, 2 * CCH)
                    for c in range(CCH):
                        if on_pool(c):
                            if c >= NPR:
                                pool.wait_ge(s_red, c - NPR + 1)
                            key_product(nc.gpsimd, c).then_inc(s_mulp, 1)
                    pool.wait_ge(s_sc, 4)
                    for c in range(CCH):
                        if on_pool(c):
                            pool.wait_ge(s_red, CCH + c - NPR + 1)
                            value_product(nc.gpsimd, c).then_inc(s_mulp, 1)

                @block.vector
                def _(dve):
                    nc.vector.tensor_copy(pm[:], con[:, bass.ds(n + C_PM, 1)]).then_inc(s_mul, 1)
                    dve.wait_ge(s_mul, 1)
                    for c in range(CCH):
                        k = 3 * c % 6
                        dve.wait_ge(s_pj, 3 * c + 2)
                        nc.vector.tensor_copy(rel[:, :, c * NPOS:(c + 1) * NPOS],
                                              ps[:, k + 1, 0:CH * NPOS].rearrange("p (h r) -> p h r", h=CH)) \
                            .then_inc(s_ed, 1)
                        dve.wait_ge(s_pj, 3 * c + 3)
                        nc.vector.tensor_scalar(kv[:, c, :, :].rearrange("p a d -> p (a d)"),
                                                ps[:, k + 2, 0:2 * P], pm[:], None, ALU.mult).then_inc(s_ed, 1)
                    dve.wait_ge(s_ev, CCH)
                    dve.wait_ge(s_ed, 2 * CCH)
                    done = 1

                    def sums(c, view, dst):
                        nonlocal done
                        if not on_pool(c):
                            dve.wait_ge(s_mul, done)
                        nc.vector.tensor_reduce(dst, prod[:, c % NPR, :].rearrange(view, h=CH, i=dst.shape[2]),
                                                AX_X, ALU.add).then_inc(s_red, 1)

                    for c in range(CCH):
                        if on_pool(c):
                            dve.wait_ge(s_mulp, c // 2 + 1)
                        else:
                            if c >= NPR:
                                dve.wait_ge(s_red, c - NPR + 1)
                            key_product(nc.vector, c).then_inc(s_mul, 1)
                            done += 1
                        sums(c, "p (h i d) -> p h i d", sc[:, :, c, :])
                    dve.wait_ge(s_red, CCH)
                    nc.vector.tensor_tensor(sc[:].rearrange("p h c k -> p h (c k)"),
                                            sc[:].rearrange("p h c k -> p h (c k)"),
                                            rel[:, :, 0:CCH * CTX], ALU.add).then_inc(s_sc, 1)
                    dve.wait_ge(s_sc, 3)
                    rows = sc[:].rearrange("p h c k -> p (h c) k")
                    nc.vector.tensor_reduce(sm[:], rows, AX_X, ALU.add).then_inc(s_sm, 1)
                    dve.wait_ge(s_sm, 1)
                    nc.vector.reciprocal(ri[:], sm[:]).then_inc(s_sm, 1)
                    dve.wait_ge(s_sm, 2)
                    nc.vector.tensor_tensor(rows, rows, ri[:].unsqueeze(2).broadcast_to([P, CH * CCH, CTX]),
                                            ALU.mult).then_inc(s_sc, 1)
                    dve.wait_ge(s_sc, 4)
                    for c in range(CCH):
                        if on_pool(c):
                            dve.wait_ge(s_mulp, CCH // 2 + c // 2 + 1)
                        else:
                            dve.wait_ge(s_red, CCH + c - NPR + 1)
                            value_product(nc.vector, c).then_inc(s_mul, 1)
                            done += 1
                        sums(c, "p (h i k) -> p h i k", ob[:, c, :].rearrange("p (h d) -> p h d", h=CH))
            clear()


def transformer(nc, t, ctx, sb0, sem, clear, con, ident, ps, xT, d_raw):
    def sb(name, shape, dt=F32):
        return sb0(name, shape, dt, ctx=ctx)

    raw = sb("raw", [P, 3 * INNER])
    wh, wl = sb("wh", [P, 3 * INNER], F32R), sb("wl", [P, 3 * INNER], F32R)
    sh, sl = sb("sh", [P, 2 * INNER], F32R), sb("sl", [P, 2 * INNER], F32R)
    wo = sb("wo", [P, HP, D])
    w1h, w1l = sb("w1h", [P, 2 * DI], F32R), sb("w1l", [P, 2 * DI], F32R)
    w2 = sb("w2", [P, NJ, D])
    svec = sb("svec", [P, 4])
    vec = sb("vec", [P, 2 + 2 * NJ + 1])
    V_G, V_B, V_B1, V_B2 = 0, 1, 2, 2 + 2 * NJ
    tab = sb("tab", [P, 4, S])
    maskb = sb("maskb", [P, 256], BF16)
    identb = sb("identb", [P, P], BF16)
    pairr = sb("pairr", [P, P], F32R)
    pairb = sb("pairb", [P, P], BF16)
    xh, xl = sb("xh", [P, S], F32R), sb("xl", [P, S], F32R)
    v = sb("v", [P, 2, TB, INNER])
    sq = sb("sq", [P, 2, S])
    sqlo = sb("sqlo", [P, 2, S], F32R)
    r1 = sb("r1", [P, 2, S])
    ra = sb("ra", [P, 2, S])
    rb = sb("rb", [P, 2, S])
    qn = sb("qn", [P, 2, S])
    kn = sb("kn", [P, 2, WIN + S])
    pr = sb("pr", [P, 2, S])
    stat = sb("stt", [P, 2, 3, 8])
    pt = sb("pt", [P, 2, S])
    on = sb("on", [P, S])
    oT = sb("oT", [P, HP, S])
    fx = sb("fx", [P, S])
    fc = sb("fc", [P, S])
    fq = sb("fq", [P, S])
    fr = sb("fr", [P, S])
    fh, fl = sb("fh", [P, S], F32R), sb("fl", [P, S], F32R)
    gx = sb("gx", [P, NJ, S])

    d_w, d_vs, d_ff = sem("d_lw"), sem("d_vs"), sem("d_ff")
    s_set, s_hi, s_lo = sem("s_set"), sem("t_hi"), sem("t_lo")
    (s_xh, s_v, s_vev, s_ab, s_sq, s_sl, s_rot, s_g, s_ssq, s_r, s_ln, s_add, s_qkn) = (
        sem(x) for x in ("t_xh", "t_v", "t_vev", "t_ab", "t_sq", "t_sl", "t_rot", "t_g", "t_ssq", "t_r", "t_ln",
                         "t_add", "t_qkn"))
    (s_S, s_m, s_sub, s_exp, s_rs, s_ri, s_pn, s_pt, s_ptev, s_o, s_oev, s_ot, s_otev) = (
        sem(x) for x in ("t_S", "t_m", "t_sub", "t_exp", "t_rs", "t_ri", "t_pn", "t_pt", "t_ptev", "t_o", "t_oev",
                         "t_ot", "t_otev"))
    (s_wo, s_x1, s_fx, s_mean, s_fc, s_fq, s_var, s_fe, s_fr, s_fn, s_fh, s_fl, s_w1, s_gx, s_gl, s_h, s_w2, s_x2) = (
        sem(x) for x in ("f_wo", "f_x1", "f_fx", "f_mean", "f_fc", "f_fq", "f_var", "f_fe", "f_fr", "f_fn", "f_fh",
                         "f_fl", "f_w1", "f_gx", "f_gl", "f_h", "f_w2", "f_x2"))
    A, BB, SS, S0, S1, TT, O0, O1 = range(8)
    swapped = raw[:, 0:2 * INNER].rearrange("p (h t d) -> p h t d", t=2, d=HALF)

    def shift_parts(act, dve, slot, hi, lo, s_hi, s_lo):
        if act:
            nc.scalar.copy(hi[0:64, :], xT[0:64, slot, :]).then_inc(s_hi, 1)
            nc.scalar.copy(hi[64:128, 1:], xT[64:128, slot, 0:S - 1]).then_inc(s_hi, 1)
        if dve:
            dve.wait_ge(s_hi, 2)
            nc.vector.tensor_tensor(lo[0:64, :], xT[0:64, slot, :], hi[0:64, :].bitcast(F32),
                                    ALU.subtract).then_inc(s_lo, 1)
            nc.vector.tensor_tensor(lo[64:128, 1:], xT[64:128, slot, 0:S - 1], hi[64:128, 1:].bitcast(F32),
                                    ALU.subtract).then_inc(s_lo, 1)

    clear()
    with nc.Block(no_gpsimd_drain=True) as block:
        @block.sync
        def _(sp):
            sp.dma_start(raw[:], t["L0_ffn_Wqkv"][0]).then_inc(d_raw, 16)

        @block.gpsimd
        def _(pool):
            zeros = (wo, w2, vec, v, qn, kn, pt, on, oT, sq, stat)
            for z in zeros:
                nc.gpsimd.memset(z[:], 0.0).then_inc(s_set, 1)
            for z in (w1h, w1l, xh, xl, sqlo):
                nc.gpsimd.memset(z[:].bitcast(F32), 0.0).then_inc(s_set, 1)
            nc.gpsimd.memset(pr[:], 1.0).then_inc(s_set, 1)
            pool.wait_ge(s_set, len(zeros) + 6)

        @block.vector
        def _(dve):
            nc.vector.memset(fx[:], 0.0).then_inc(s_hi, 1)
            nc.vector.memset(gx[:], 0.0).then_inc(s_hi, 1)
            nc.vector.memset(xT[:, B, :], 0.0).then_inc(s_hi, 1)
            nc.vector.tensor_copy(maskb[:], con[:, C_MASK:C_MASK + 256]).then_inc(s_hi, 1)
            nc.vector.tensor_copy(identb[:], ident).then_inc(s_hi, 1)
            nc.vector.tensor_copy(pairr[:], con[:, C_PAIR:C_PAIR + P]).then_inc(s_hi, 1)
            nc.vector.tensor_copy(pairb[:], con[:, C_PAIR:C_PAIR + P]).then_inc(s_hi, 1)
            dve.wait_ge(s_hi, 7)
    clear()
    with nc.Block(no_gpsimd_drain=True) as block:
        @block.scalar
        def _(act):
            shift_parts(act, None, 0, xh, xl, s_hi, s_lo)

        @block.vector
        def _(dve):
            shift_parts(None, dve, 0, xh, xl, s_hi, s_lo)
            dve.wait_ge(s_lo, 2)
    clear()

    def attention_weights(l):
        with nc.Block(no_gpsimd_drain=True) as block:
            @block.sync
            def _(sp):
                sp.dma_start(tab[:], t["rotary"]).then_inc(d_w, 16)
                for i, n in ((0, "L0_ffn_q_scale"), (2, "L0_ffn_k_scale")):
                    src = t[n].rearrange("l (d o) -> l d o", o=1)
                    for g in range(4):
                        own, other = (g % 2) * HALF, (1 - g % 2) * HALF
                        sp.dma_start(svec[g * HALF:(g + 1) * HALF, i:i + 1], src[l, own:own + HALF]).then_inc(d_w, 16)
                        sp.dma_start(svec[g * HALF:(g + 1) * HALF, i + 1:i + 2],
                                     src[l, other:other + HALF]).then_inc(d_w, 16)

            @block.scalar
            def _(act):
                act.wait_ge(d_raw, 16)
                nc.scalar.copy(wh[:], raw[:]).then_inc(s_hi, 1)
                for a in range(2):
                    nc.scalar.copy(sh[:].rearrange("p (h t d) -> p h t d", t=2, d=HALF)[:, :, a, :],
                                   swapped[:, :, 1 - a, :]).then_inc(s_hi, 1)

            @block.vector
            def _(dve):
                dve.wait_ge(s_hi, 1)
                nc.vector.tensor_tensor(wl[:], raw[:], wh[:].bitcast(F32), ALU.subtract).then_inc(s_lo, 1)
                dve.wait_ge(s_hi, 3)
                for a in range(2):
                    nc.vector.tensor_tensor(
                        sl[:].rearrange("p (h t d) -> p h t d", t=2, d=HALF)[:, :, a, :], swapped[:, :, 1 - a, :],
                        sh[:].bitcast(F32).rearrange("p (h t d) -> p h t d", t=2, d=HALF)[:, :, a, :],
                        ALU.subtract).then_inc(s_lo, 1)
                dve.wait_ge(d_w, 16 * 17)
                for i in range(4):
                    nc.vector.tensor_scalar(tab[:, i, :], tab[:, i, :], svec[:, i:i + 1], None,
                                            ALU.mult).then_inc(s_lo, 1)
                dve.wait_ge(s_lo, 7)
        nc.sync.sem_clear(d_raw)
        clear()

    def feed_forward_weights(l):
        w1raw = raw[:, 0:2 * DI]
        with nc.Block(no_gpsimd_drain=True) as block:
            @block.sync
            def _(sp):
                sp.dma_start(wo[:], t["L0_ffn_Wo"][l].rearrange("(a p) n -> p a n", p=P)).then_inc(d_w, 16)
                sp.dma_start(w1raw, t["L0_ffn_W1"][l]).then_inc(d_w, 16)
                for j in range(NJ):
                    sp.dma_start(w2[0:JW[j], j, :], t["L0_ffn_W2"][l, j * P:j * P + JW[j], :]).then_inc(d_w, 16)
                sp.wait_ge(d_w, 16 * (2 + NJ))
                sp.wait_ge(s_lo, 1)
                sp.dma_start(raw[:], t["L0_ffn_Wqkv"][(l + 1) % DEPTH]).then_inc(d_raw, 16)

            @block.scalar
            def _(act):
                for i, n in ((V_G, "L0_ffn_ln_g"), (V_B, "L0_ffn_ln_b"), (V_B2, "L0_ffn_b2")):
                    act.dma_start(vec[:, i:i + 1], t[n].rearrange("l (d o) -> l d o", o=1)[l]).then_inc(d_ff, 16)
                b1 = t["L0_ffn_b1"].rearrange("l (d o) -> l d o", o=1)
                for a in range(2):
                    for j in range(NJ):
                        c = V_B1 + a * NJ + j
                        o = a * DI + j * P
                        act.dma_start(vec[0:JW[j], c:c + 1], b1[l, o:o + JW[j]]).then_inc(d_ff, 16)
                act.wait_ge(d_w, 16 * (2 + NJ))
                nc.scalar.copy(w1h[:], w1raw).then_inc(s_hi, 1)
                act.wait_ge(d_ff, 16 * (3 + 2 * NJ))

            @block.vector
            def _(dve):
                dve.wait_ge(s_hi, 1)
                nc.vector.tensor_tensor(w1l[:], w1raw, w1h[:].bitcast(F32), ALU.subtract).then_inc(s_lo, 1)
        clear()

    V_AT = [(0, 0, O0), (0, 0, O1), (0, 1, SS), (1, 0, O0), (2, 0, O0), (2, 0, O1), (3, 0, O1), (4, 0, O0)]

    def round_(pb, nb, drain=False):
        full = not drain

        def live(i, lag):
            return full or i < lag

        def before(i, lag):
            return i if full else min(i, lag)

        def after(eng, s, n):
            if n > 0:
                eng.wait_ge(s, n)

        def v_chunks(i, end):
            return [j for j in range(8) if full and V_AT[j][:2] == (i, end)]

        with nc.Block(no_gpsimd_drain=True) as block:
            @block.tensor
            def _(pe):
                def three(dst, ah, al, bh, bl):
                    nc.tensor.matmul(dst, al, bh, start=True, stop=False)
                    nc.tensor.matmul(dst, ah, bl, start=False, stop=False)
                    return nc.tensor.matmul(dst, ah, bh, start=False, stop=True)

                def project(i, k):
                    after(pe, s_rot, 2 * i + k)
                    c = k * INNER + i * P
                    three(ps[:, A, :], wh[:, c:c + P], wl[:, c:c + P], xh[:], xl[:])
                    three(ps[:, BB, :], sh[:, c:c + P], sl[:, c:c + P], xh[:], xl[:]).then_inc(s_ab, 1)

                def squares(i, k):
                    after(pe, s_sl, 2 * i if k else 2 * i + 1)
                    after(pe, s_g, 2 * i if k else 2 * i + 1)
                    nc.tensor.matmul(ps[:, SS, :], pairr[:], sqlo[:, k, :], start=True, stop=False)
                    nc.tensor.matmul(ps[:, SS, :], pairb[:], sq[:, k, :].bitcast(BF16)[:, 1::2],
                                     start=False, stop=True).then_inc(s_ssq, 1)

                def values_of(j):
                    hf, tb, bank = j // 4, j % 4, V_AT[j][2]
                    c = 2 * INNER + 512 * hf
                    three(ps[:, bank, :], xh[:, tb * P:(tb + 1) * P], xl[:, tb * P:(tb + 1) * P],
                          wh[:, c:c + 512], wl[:, c:c + 512]).then_inc(s_v, 1)

                def scores(i):
                    after(pe, s_sub, before(i, 1))
                    for e in range(2):
                        nc.tensor.matmul(ps[:, S0 + e, 0:256], identb[:], maskb[:], start=True, stop=False,
                                         skip_group_check=True)
                    pe.wait_ge(s_qkn, 2 * i + 1)
                    for e in range(2):
                        q = qn[e * DH:(e + 1) * DH, (i - 1) % 2, :]
                        k = kn[e * DH:(e + 1) * DH, (i - 1) % 2, :]
                        for wd in range(S // WIN):
                            tb, whi, wlo = wd // 4, wd // 2 % 2, wd % 2
                            strip = (tb % 2 * 2 + wlo) * WIN
                            col = (tb // 2 * 2 + whi) * 2 * WIN
                            last = nc.tensor.matmul(
                                ps[strip:strip + WIN, S0 + e, col:col + 2 * WIN], q[:, wd * WIN:(wd + 1) * WIN],
                                k[:, wd * WIN:(wd + 2) * WIN], start=False, stop=True, skip_group_check=True,
                                tile_position=(e * DH, strip))
                    last.then_inc(s_S, 1)

                def turn_probs(i):
                    pe.wait_ge(s_pn, i + 1)
                    if live(i, 3):
                        pe.wait_ge(s_otev, i + 1)
                    for m in range(4):
                        last = nc.tensor.transpose(ps[:, TT, m * P:(m + 1) * P],
                                                   pr[:, i % 2, m * P:(m + 1) * P], ident)
                    last.then_inc(s_pt, 1)

                def values(i):
                    pe.wait_ge(s_ptev, i + 1)
                    after(pe, s_oev, before(i, 2))
                    if full:
                        after(pe, s_vev, (2, 4, 6, 7, 8, 8, 8, 8)[i])
                        if i in (2, 6):
                            pe.wait_ge(d_vs, 32 if i == 2 else 64)
                        for step, s, n in ((3, s_fc, 1), (5, s_gx, 2), (6, s_h, 2), (7, s_x2, 1)):
                            if i == step:
                                pe.wait_ge(s, n)
                    hp = (i - 2) % HP
                    for whi in range(2):
                        for tb in range(TB):
                            for wlo in range(2):
                                for e in range(2):
                                    strip = (tb % 2 * 2 + wlo) * WIN
                                    c = (e * 2 + tb // 2) * P + strip
                                    o = (tb // 2) * P + e * DH
                                    hh = 2 * hp + e
                                    last = nc.tensor.matmul(
                                        ps[strip:strip + WIN, O0 + whi, o:o + DH],
                                        pt[whi * DH:(whi + 1) * DH, i % 2, c:c + WIN],
                                        v[whi * DH:(whi + 1) * DH, 1 - wlo, tb, hh * DH:(hh + 1) * DH],
                                        start=True, stop=True, skip_group_check=True,
                                        tile_position=(whi * DH, strip))
                    last.then_inc(s_o, 1)

                def turn_out(i):
                    after(pe, s_oev, before(i, 2))
                    after(pe, s_ptev, before(i, 2))
                    for m in range(4):
                        last = nc.tensor.transpose(ps[:, TT, m * P:(m + 1) * P], on[:, m * P:(m + 1) * P], ident)
                    last.then_inc(s_ot, 1)

                def up(a, j, bank):
                    c = a * DI + j * P
                    three(ps[0:JW[j], bank, :], w1h[:, c:c + JW[j]], w1l[:, c:c + JW[j]], fh[:], fl[:]) \
                        .then_inc(s_w1, 1)

                def middle(i):
                    if i == 3:
                        pe.wait_ge(s_fx, 2)
                    if v_chunks(i, 0) or i in (3, 5, 6, 7):
                        after(pe, s_oev, before(i, 2))
                    if i == 3:
                        nc.tensor.matmul(ps[:, O0, :], con[:, C_MEAN:C_MEAN + P], fx[:], start=True,
                                         stop=True).then_inc(s_mean, 1)
                    for j in v_chunks(i, 0):
                        values_of(j)
                    if i == 5:
                        pe.wait_ge(s_fh, 1)
                        pe.wait_ge(s_fl, 1)
                        up(1, 0, O0)
                        up(1, 1, O1)
                    if i == 6:
                        pe.wait_ge(s_gx, 2)
                        up(0, 0, O0)
                        up(0, 1, O1)
                    if i == 7:
                        pe.wait_ge(s_h, 3)
                        for j in range(NJ):
                            last = nc.tensor.matmul(ps[:, O0, :], w2[0:JW[j], j, :], gx[0:JW[j], j, :],
                                                    start=(j == 0), stop=(j == NJ - 1))
                        last.then_inc(s_w2, 1)

                def end(i):
                    if v_chunks(i, 1) or i in (2, 3, 5, 6):
                        pe.wait_ge(s_g, 2 * i + 2 if full else 1)
                    for j in v_chunks(i, 1):
                        values_of(j)
                    if i == 2:
                        pe.wait_ge(s_otev, 3)
                        for p in range(HP):
                            last = nc.tensor.matmul(ps[:, SS, :], wo[:, p, :], oT[:, p, :], start=(p == 0),
                                                    stop=(p == HP - 1))
                        last.then_inc(s_wo, 1)
                    if i == 3:
                        pe.wait_ge(s_fq, 1)
                        nc.tensor.matmul(ps[:, SS, :], con[:, C_MEAN:C_MEAN + P], fq[:], start=True,
                                         stop=True).then_inc(s_var, 1)
                    if i == 5:
                        pe.wait_ge(s_fe, 1)
                        up(1, 2, SS)
                    if i == 6:
                        pe.wait_ge(s_gx, 3)
                        up(0, 2, SS)

                for i in range(HP):
                    if full:
                        project(i, 0)
                    if live(i, 3):
                        turn_out(i)
                    if full:
                        for step, s, n in ((1, s_vev, 3), (3, s_x1, 1), (4, s_fe, 1), (6, s_gx, 3), (7, s_h, 3)):
                            if i == step:
                                pe.wait_ge(s, n)
                    if live(i, 1):
                        squares(i, 1)
                    middle(i)
                    if full:
                        project(i, 1)
                    if live(i, 2):
                        turn_probs(i)
                    if full:
                        squares(i, 0)
                    if live(i, 1):
                        scores(i)
                    if live(i, 2):
                        values(i)
                    end(i)

            @block.scalar
            def _(act):
                nc.scalar.preload_act_table_set(LN_EXP)

                def square(i, k):
                    n = 2 * i + k
                    act.wait_ge(s_ab, n + 1)
                    after(act, s_ssq, 2 * i + k)
                    nc.scalar.activation(sq[:, k, :], ps[:, A, :], ACT.Square).then_inc(s_sq, 1)

                def inverse_norm(i, k):
                    n = 2 * i + 1 if k else 2 * i + 2
                    act.wait_ge(s_g, n)
                    nc.scalar.activation(r1[:, k, :], r1[:, k, :], ACT.Ln, scale=RN * RN).then_inc(s_ln, 1)
                    act.wait_ge(s_ln, n)
                    nc.scalar.activation(r1[:, k, :], r1[:, k, :], ACT.Exp, scale=-0.5).then_inc(s_r, 1)

                def values_read(j):
                    act.wait_ge(s_v, j + 1)
                    if j == 4:
                        act.wait_ge(s_o, 2)
                    hf, tb = j // 4, j % 4
                    nc.scalar.copy(v[:, 0, tb, hf * 512:(hf + 1) * 512], ps[:, V_AT[j][2], :]).then_inc(s_vev, 1)

                def gate(j, bank):
                    m = JW[j]
                    act.wait_ge(s_w1, j + 1)
                    nc.scalar.activation(gx[0:m, j, :], ps[0:m, bank, :], ACT.Identity,
                                         bias=vec[0:m, V_B1 + NJ + j:V_B1 + NJ + j + 1]).then_inc(s_gx, 1)

                for i in range(HP):
                    if full:
                        square(i, 0)
                    if live(i, 3):
                        act.wait_ge(s_ot, i + 1)
                        nc.scalar.copy(oT_view(oT, (i - 3) % HP),
                                       ps[:, TT, :].rearrange("p (wh t2 t1 s) -> p wh t2 t1 s", wh=2, t2=2, t1=2)) \
                           .then_inc(s_otev, 1)
                    if i == 4:
                        act.wait_ge(s_fe, 1)
                        nc.scalar.activation(fr[:], fr[:], ACT.Ln).then_inc(s_fr, 1)
                        act.wait_ge(s_fr, 1)
                        nc.scalar.activation(fr[:], fr[:], ACT.Exp, scale=-0.5).then_inc(s_fr, 1)
                    if live(i, 1):
                        inverse_norm(i, 1)
                    for j in v_chunks(i, 0):
                        values_read(j)
                    if i == 3:
                        act.wait_ge(s_fc, 1)
                        nc.scalar.activation(fq[:], fc[:], ACT.Square).then_inc(s_fq, 1)
                    if i == 5:
                        gate(0, O0)
                        gate(1, O1)
                    if full:
                        square(i, 1)
                    if live(i, 2):
                        act.wait_ge(s_pt, i + 1)
                        after(act, s_o, i - 1)
                        nc.scalar.copy(pt[:, i % 2, :], ps[:, TT, :]).then_inc(s_ptev, 1)
                    if full:
                        inverse_norm(i, 0)
                    if i == 4:
                        act.wait_ge(s_fn, 2)
                        nc.scalar.copy(fh[:], fc[:]).then_inc(s_fh, 1)
                    if i == HP - 1 and full:
                        act.wait_ge(s_ab, 2 * HP)
                        shift_parts(act, None, nb, xh, xl, s_xh, None)
                    if live(i, 1):
                        act.wait_ge(s_sub, i + 1)
                        nc.scalar.activation(pr[:, (i - 1) % 2, :], pr[:, (i - 1) % 2, :], ACT.Exp).then_inc(s_exp, 1)
                    if live(i, 2):
                        act.wait_ge(s_o, i + 1)
                        if live(i, 3):
                            act.wait_ge(s_ot, i + 1)
                        nc.scalar.copy(on[:].rearrange("p (w c) -> p w c", w=2), ps[:, O0:O1 + 1, 0:256]) \
                            .then_inc(s_oev, 1)
                    for j in v_chunks(i, 1):
                        values_read(j)
                    if i == 5:
                        gate(2, SS)
                        act.wait_ge(s_gx, NJ)
                        nc.scalar.activation(gx[:], gx[:], ACT.Gelu).then_inc(s_gl, 1)
                        nc.scalar.preload_act_table_set(LN_EXP)

            @block.gpsimd
            def _(pool):
                def rotate(i, k):
                    n = 2 * i + k
                    pool.wait_ge(s_rot, n + 1)
                    after(pool, s_S, i)
                    dst = kn[:, i % 2, WIN:] if k else qn[:, i % 2, :]
                    nc.gpsimd.tensor_tensor(dst, ra[:, k, :], rb[:, k, :], ALU.add).then_inc(s_add, 1)

                def normalise(i, k):
                    dst = kn[:, (i - 1) % 2, WIN:] if k else qn[:, i % 2, :]
                    after(pool, s_add, 2 * i if k else 2 * i + 1)
                    pool.wait_ge(s_r, 2 * i + 1 if k else 2 * i + 2)
                    nc.gpsimd.tensor_tensor(dst, dst, r1[:, k, :], ALU.mult).then_inc(s_qkn, 1)

                for i in range(HP):
                    if live(i, 2):
                        pool.wait_ge(s_ri, i + 1)
                        p3 = pr[:, i % 2, :].rearrange("p (g k) -> p g k", g=8)
                        nc.gpsimd.tensor_tensor(p3, p3, stat[:, i % 2, 2, :].unsqueeze(2)
                                                .broadcast_to([P, 8, 64]), ALU.mult).then_inc(s_pn, 1)
                    if full:
                        rotate(i, 0)
                    if live(i, 1):
                        normalise(i, 1)
                    if full:
                        rotate(i, 1)
                        normalise(i, 0)
                pool.wait_ge(s_pn, HP if full else 2)
                pool.wait_ge(s_qkn, 2 * HP if full else 1)

            @block.sync
            def _(sp):
                for hf in range(2 if full else 0):
                    c = slice(512 * hf, 512 * hf + 512)
                    sp.wait_ge(s_vev, 4 * hf + 4)
                    if hf:
                        sp.wait_ge(s_o, 2)
                    sp.dma_start(v[WIN:P, 1, :, c], v[0:P - WIN, 0, :, c]).then_inc(d_vs, 16)
                    sp.dma_start(v[0:WIN, 1, 1:TB, c], v[P - WIN:P, 0, 0:TB - 1, c]).then_inc(d_vs, 16)
                if full:
                    sp.wait_ge(d_vs, 64)

            @block.vector
            def _(dve):
                def rotary(i, k):
                    n = 2 * i + k
                    dve.wait_ge(s_sq, n + 1)
                    after(dve, s_ssq, 2 * i + k)
                    nc.vector.tensor_tensor(sqlo[:, k, :], sq[:, k, :], sq[:, k, :].bitcast(BF16)[:, 1::2],
                                            ALU.subtract).then_inc(s_sl, 1)
                    after(dve, s_add, n - 1)
                    nc.vector.tensor_tensor(rb[:, k, :], ps[:, BB, :], tab[:, 2 * k + 1, :], ALU.mult)
                    nc.vector.tensor_tensor(ra[:, k, :], ps[:, A, :], tab[:, 2 * k, :], ALU.mult).then_inc(s_rot, 1)

                def guard(i, k):
                    dve.wait_ge(s_ssq, 2 * i + 1 if k else 2 * i + 2)
                    after(dve, s_qkn, 2 * i - 1 if k else 2 * i)
                    nc.vector.tensor_scalar(r1[:, k, :], ps[:, SS, :], 1e-24, None, ALU.max).then_inc(s_g, 1)

                def subtract_max(i):
                    b = (i - 1) % 2
                    dve.wait_ge(s_S, i + 1)
                    s4 = ps[:, S0:S1 + 1, 0:256].rearrange("p e (g k) -> p e g k", g=4)
                    after(dve, s_pt, before(i, 2))
                    nc.vector.tensor_reduce(stat[:, b, 0, :].rearrange("p (e g) -> p e g", e=2), s4, AX_X,
                                            ALU.max).then_inc(s_m, 1)
                    dve.wait_ge(s_m, i + 1)
                    nc.vector.tensor_tensor(pr[:, b, :].rearrange("p (e g k) -> p e g k", e=2, g=4), s4,
                                            stat[:, b, 0, :].rearrange("p (e g) -> p e g", e=2).unsqueeze(3)
                                            .broadcast_to([P, 2, 4, 64]), ALU.subtract).then_inc(s_sub, 1)

                def row_sums(i):
                    b = i % 2
                    after(dve, s_exp, i)
                    nc.vector.tensor_reduce(stat[:, b, 1, :], pr[:, b, :].rearrange("p (g k) -> p g k", g=8),
                                            AX_X, ALU.add).then_inc(s_rs, 1)
                    dve.wait_ge(s_rs, i + 1)
                    nc.vector.reciprocal(stat[:, b, 2, :], stat[:, b, 1, :]).then_inc(s_ri, 1)

                def gated(j, bank):
                    m = JW[j]
                    dve.wait_ge(s_gl, 1)
                    dve.wait_ge(s_w1, NJ + j + 1)
                    nc.vector.scalar_tensor_tensor(out=gx[0:m, j, :], in0=ps[0:m, bank, :],
                                                   scalar=vec[0:m, V_B1 + j:V_B1 + j + 1], in1=gx[0:m, j, :],
                                                   op0=ALU.add, op1=ALU.mult).then_inc(s_h, 1)

                for i in range(HP):
                    if live(i, 2):
                        row_sums(i)
                    if full:
                        rotary(i, 0)
                    if live(i, 1):
                        guard(i, 1)
                    if i == 3:
                        dve.wait_ge(s_mean, 1)
                        nc.vector.tensor_tensor(fc[:], fx[:], ps[:, O0, :], ALU.subtract).then_inc(s_fc, 1)
                    if i == 4:
                        dve.wait_ge(s_fr, 2)
                        nc.vector.tensor_tensor(fc[:], fc[:], fr[:], ALU.mult).then_inc(s_fn, 1)
                    if i == 6:
                        gated(0, O0)
                        gated(1, O1)
                    if i == 7:
                        dve.wait_ge(s_w2, 1)
                        nc.vector.scalar_tensor_tensor(out=xT[:, pb, :], in0=ps[:, O0, :],
                                                       scalar=vec[:, V_B2:V_B2 + 1], in1=xT[:, pb, :],
                                                       op0=ALU.add, op1=ALU.add).then_inc(s_x2, 1)
                    if full:
                        rotary(i, 1)
                    if i == 4:
                        dve.wait_ge(s_fn, 1)
                        nc.vector.tensor_scalar(fc[:], fc[:], vec[:, V_G:V_G + 1], vec[:, V_B:V_B + 1],
                                                ALU.mult, ALU.add).then_inc(s_fn, 1)
                    if full:
                        guard(i, 0)
                    if live(i, 1):
                        subtract_max(i)
                    if i == 4:
                        dve.wait_ge(s_fh, 1)
                        nc.vector.tensor_tensor(fl[:], fc[:], fh[:].bitcast(F32), ALU.subtract).then_inc(s_fl, 1)
                    if i == 2:
                        dve.wait_ge(s_wo, 1)
                        nc.vector.tensor_tensor(xT[:, pb, :], ps[:, SS, :], xT[:, pb, :], ALU.add).then_inc(s_x1, 1)
                        dve.wait_ge(s_x1, 1)
                        nc.vector.tensor_copy(fx[0:64, :], xT[0:64, pb, :]).then_inc(s_fx, 1)
                        nc.vector.tensor_copy(fx[64:128, 1:], xT[64:128, pb, 0:S - 1]).then_inc(s_fx, 1)
                    if i == 3:
                        dve.wait_ge(s_var, 1)
                        nc.vector.tensor_scalar(fr[:], ps[:, SS, :], EPS, None, ALU.add).then_inc(s_fe, 1)
                    if i == 6:
                        gated(2, SS)
                if full:
                    shift_parts(None, dve, nb, xh, xl, s_xh, s_xh)
                    dve.wait_ge(s_xh, 4)
                dve.wait_ge(s_x2, 1)
        clear()

    with nc.Fori(0, DEPTH) as l:
        attention_weights(l)
        round_(B - 1 + ((B - l) >> 3), 1)
        feed_forward_weights(l)
        with nc.Fori(1, B) as b:
            round_(b - 1, (b + 1) % B)
    round_(B - 1, None, drain=True)


def oT_view(oT, i):
    return oT[:, i, :].rearrange("p (t2 t1 wh s) -> p wh t2 t1 s", t2=2, t1=2, wh=2)


_INS = ['L0_attn_hidden_states', 'L0_attn_position_embeddings', 'L0_attn_Wq', 'L0_attn_Wk', 'L0_attn_Wv',
        'L0_attn_Wpost', 'L0_attn_Wrel', 'L0_attn_per_dim_scale', 'L0_ffn_Wqkv', 'L0_ffn_q_scale',
        'L0_ffn_k_scale', 'L0_ffn_Wo', 'L0_ffn_ln_g', 'L0_ffn_ln_b', 'L0_ffn_W1', 'L0_ffn_b1', 'L0_ffn_W2',
        'L0_ffn_b2']


def kernel(**inputs):
    import concourse.bacc as bacc
    from concourse.bass_utils import run_bass_kernel_spmd

    nc = bacc.Bacc("TRN2", target_bir_lowering=False, num_devices=1)
    arrays, args = {}, {}
    given = {**inputs, "consts": constants(), "rotary": rotary_tables()}
    for name in _INS + ["consts", "rotary"]:
        a = np.ascontiguousarray(given[name])
        arrays[f"in_{name}"] = a
        args[name] = nc.dram_tensor(f"in_{name}", a.shape, mybir.dt.from_np(a.dtype), kind="ExternalInput").ap()
    out = nc.dram_tensor("out_0", (B, S, D), F32, kind="ExternalOutput").ap()
    build(nc, args, out)
    r = run_bass_kernel_spmd(nc, [arrays], core_ids=[0])
    return r.results[0]["out_0"]
```

```python
import math
from contextlib import ExitStack

import numpy as np

import concourse.bass as bass
from concourse import mybir

ALU = mybir.AluOpType
ACT = mybir.ActivationFunctionType
F32 = mybir.dt.float32
BF16 = mybir.dt.bfloat16
F32R = mybir.dt.float32r
AX_X = mybir.AxisListType.X

P = 128
B, S, D = 8, 512, 128
TB = S // P
EPS = 1e-5

CH, CCH, CD = 8, 12, 16
CTX = 2 * CCH
NPOS = CTX + 1
NB = -(-S // CCH)
SP = NB * CCH
NTILE = -(-B * NB // P)
TW = P * CCH
SOFTCAP = 50.0
Q_SCALE = CD ** -0.5 / math.log(2)
K_SCALE = math.log(1.0 + math.e) / math.log(2)

DEPTH, HEADS, DH, WIN = 6, 16, 64, 32
INNER = HEADS * DH
HP = HEADS // 2
HALF = DH // 2
DI = int(D * 4 * 2 / 3)
NJ = -(-DI // P)
JW = [min(P, DI - P * j) for j in range(NJ)]
NEG = -1e30
LN_EXP = "natural_log_exp_and_others"
RN = 256.0

C_ID, C_MASK, C_PAIR, C_MEAN, C_HM, C_PM = 0, 128, 384, 512, 640, 648
C_END = C_PM + NTILE


def constants():
    c = np.zeros((P, C_END), np.float32)
    c[:, C_ID:C_ID + P] = np.eye(P)
    i = np.arange(P) % WIN
    j = np.arange(2 * WIN)
    ok = (j[None] >= i[:, None]) & (j[None] <= i[:, None] + WIN)
    mask = np.tile(np.where(ok, 0.0, NEG), (1, 4)).astype(np.float32)
    mask[0:WIN, 0:WIN] = NEG
    c[:, C_MASK:C_MASK + 256] = mask
    p = np.arange(P)
    c[:, C_PAIR:C_PAIR + P] = p[:, None] // DH == p[None] // DH
    c[:, C_MEAN:C_MEAN + P] = 1.0 / D
    c[:, C_HM:C_HM + CH] = p[:, None] // CD == np.arange(CH)[None]
    for n in range(NTILE):
        c[:, C_PM + n] = (n * P + p) % NB != 0
    return c


def rotary_tables():
    f = np.float32
    half = np.arange(0, DH, 2, dtype=f)
    inv_freq = (f(1.0) / f(10000.0) ** (half / f(DH))).astype(f)
    t = np.arange(S, dtype=f)
    freqs = t[:, None] * inv_freq[None]
    base = (half + f(0.4 * DH)) / f(1.4 * DH)
    power = ((t - S // 2) / f(WIN // 2)).astype(f)
    scale = base[None] ** power[:, None]
    cos, sin = np.cos(freqs), np.sin(freqs)
    sign = np.where(np.arange(P) % DH < HALF, -1.0, 1.0).astype(f)[:, None]
    four = lambda a: np.tile(a.T, (4, 1)).astype(f)
    tables = (8 * RN * four(cos * scale), 8 * RN * four(sin * scale) * sign,
              RN * four(cos / scale), RN * four(sin / scale) * sign)
    return np.stack(tables, axis=1).astype(f)


def build(nc, t, out):
    with ExitStack() as top:
        def sb(name, shape, dt=F32, ctx=top):
            return ctx.enter_context(nc.sbuf_tensor(name, shape, dt))

        sems = []

        def sem(name, keep=False):
            s = top.enter_context(nc.semaphore(name))
            if not keep:
                sems.append(s.num)
            return s

        ps = top.enter_context(nc.psum_tensor("ps", [P, 8, 512], F32))
        con = sb("con", [P, C_END])
        xT = sb("xT", [P, B + 1, S])
        sT = nc.dram_tensor("sT", (P, NTILE * TW), F32, kind="Internal").ap()
        ident = con[:, C_ID:C_ID + P]

        d_raw, d_ff = sem("d_raw", keep=True), sem("d_ff", keep=True)
        d_in, d_out = sem("d_in"), sem("d_out")

        def clear():
            nc.sync.sem_clear(range(min(sems), max(sems) + 1))
            nc.all_engine_barrier()

        clear()

        conf = ExitStack()
        cx = sb("cx", [P, CCH + NTILE * TW], ctx=conf)
        s_zero, s_stat, s_var, s_rs, s_xn, s_tr, s_xt = (
            sem("s_zero"), sem("s_stat"), sem("s_var"), sem("s_rs"), sem("s_xn"), sem("s_tr"), sem("s_xt"))
        with ExitStack() as ctx:
            xnat = sb("xnat", [P, B, TB, D], ctx=ctx)
            stat = sb("stat", [P, B, TB, 6], ctx=ctx)
            mv = sb("mv", [P, B, TB, 2], ctx=ctx)
            lnv = sb("lnv", [P, B * TB], ctx=ctx)
            rstd = sb("rstd", [P, B, TB], ctx=ctx)
            with nc.Block(no_gpsimd_drain=True) as block:
                @block.sync
                def _(sp):
                    with sp.Fori(0, B) as b:
                        sp.dma_start(xnat[:, b], t["L0_attn_hidden_states"].rearrange(
                            "b (t p) d -> p b t d", p=P)[:, b]).then_inc(d_in, 16)
                    sp.dma_start(con[:], t["consts"]).then_inc(d_out, 16)

                @block.gpsimd
                def _(pool):
                    nc.gpsimd.memset(cx[:], 0.0).then_inc(s_zero, 1)
                    pool.wait_ge(s_zero, 1)

                @block.vector
                def _(dve):
                    dve.wait_ge(d_in, 16 * B)
                    with dve.Fori(0, B) as b:
                        for k in range(TB):
                            nc.vector.bn_stats(stat[:, b, k, :], xnat[:, b, k, :]).then_inc(s_stat, 1)
                    dve.wait_ge(s_stat, B * TB)
                    for b in range(B):
                        for k in range(TB):
                            nc.vector.bn_aggr(mv[:, b, k, :], stat[:, b, k, :]).then_inc(s_stat, 1)
                    dve.wait_ge(s_stat, 2 * B * TB)
                    nc.vector.tensor_scalar(lnv[:], mv[:].rearrange("p b t s -> p (b t) s")[:, :, 1], EPS, None,
                                            ALU.add).then_inc(s_var, 1)
                    dve.wait_ge(s_rs, 1)
                    with dve.Fori(0, B) as b:
                        for k in range(TB):
                            nc.vector.tensor_scalar(xnat[:, b, k, :], xnat[:, b, k, :], mv[:, b, k, 0:1],
                                                    rstd[:, b, k:k + 1], ALU.subtract, ALU.mult).then_inc(s_xn, 1)

                @block.scalar
                def _(act):
                    act.wait_ge(s_var, 1)
                    nc.scalar.activation(lnv[:], lnv[:], ACT.Ln).then_inc(s_var, 1)
                    act.wait_ge(s_var, 2)
                    nc.scalar.activation(rstd[:].rearrange("p b t -> p (b t)"), lnv[:], ACT.Exp,
                                         scale=-0.5).then_inc(s_rs, 1)
                    act.wait_ge(s_zero, 1)
                    with act.Fori(0, B) as b:
                        act.wait_ge(s_tr, b + 1)
                        nc.scalar.copy(xT[:, b, :], ps[:, b, :])
                        nc.scalar.copy(cx[:, bass.ds(b * SP + CCH, S)], ps[:, b, :]).then_inc(s_xt, 1)
                    act.wait_ge(s_xt, B)

                @block.tensor
                def _(pe):
                    pe.wait_ge(d_out, 16)
                    for b in range(B):
                        pe.wait_ge(s_xn, TB * b + TB)
                        for k in range(TB):
                            last = nc.tensor.transpose(ps[:, b, k * P:(k + 1) * P], xnat[:, b, k, :], ident)
                        last.then_inc(s_tr, 1)
            clear()

        with conf:
            chunked_attention(nc, t, conf, sb, sem, clear, con, ident, ps, cx, sT)

        with ExitStack() as ctx:
            transformer(nc, t, ctx, sb, sem, clear, con, ident, ps, xT, d_raw, d_ff)

        s_z, s_y, s_t4, s_o = sem("s_z"), sem("s_y"), sem("s_t4"), sem("s_o")
        with ExitStack() as ctx:
            d_s = sem("d_s")
            srow = sb("srow", [P, B, S], ctx=ctx)
            z = sb("z", [P, B, S], ctx=ctx)
            xrow = sb("xrow", [P, B, TB, D], ctx=ctx)
            clear()
            with nc.Block(no_gpsimd_drain=True) as block:
                @block.sync
                def _(sp):
                    with sp.Fori(0, B) as b:
                        sp.dma_start(srow[:, b], sT[:, bass.ds(b * SP, S)]).then_inc(d_s, 16)
                    with sp.Fori(0, B) as b:
                        sp.dma_start(xrow[:, b], t["L0_attn_hidden_states"].rearrange(
                            "b (t p) d -> p b t d", p=P)[:, b]).then_inc(d_in, 16)
                    with sp.Fori(0, B) as b:
                        sp.wait_ge(s_o, b + 1)
                        sp.dma_start(out.rearrange("b (t p) d -> p b t d", p=P)[:, b], xrow[:, b]).then_inc(d_out, 16)
                    sp.wait_ge(d_out, 16 * B)

                @block.scalar
                def _(act):
                    with act.Fori(0, B) as b:
                        nc.scalar.activation(z[:, b], xT[:, b, :], ACT.Silu).then_inc(s_z, 1)

                @block.vector
                def _(dve):
                    dve.wait_ge(d_s, 16 * B)
                    with dve.Fori(0, B) as b:
                        dve.wait_ge(s_z, b + 1)
                        nc.vector.tensor_tensor(z[:, b], srow[:, b], z[:, b], ALU.mult).then_inc(s_y, 1)
                    dve.wait_ge(d_in, 16 * B)
                    with dve.Fori(0, B) as b:
                        dve.wait_ge(s_t4, b + 1)
                        nc.vector.tensor_tensor(xrow[:, b], ps[:, b, :].rearrange("p (t d) -> p t d", t=TB),
                                                xrow[:, b], ALU.add).then_inc(s_o, 1)

                @block.tensor
                def _(pe):
                    for b in range(B):
                        pe.wait_ge(s_y, b + 1)
                        for k in range(TB):
                            last = nc.tensor.transpose(ps[:, b, k * P:(k + 1) * P], z[:, b, k * P:(k + 1) * P], ident)
                        last.then_inc(s_t4, 1)


def chunked_attention(nc, t, ctx0, sb, sem, clear, con, ident, ps, cx, sT):
    d_st = sem("d_st")
    d_w, s_sp, s_ws, s_wt, s_we, s_re = (
        sem("d_w"), sem("s_sp"), sem("s_ws"), sem("s_wt"), sem("s_we"), sem("s_re"))
    with ExitStack() as ctx:
        names = ["L0_attn_Wq", "L0_attn_Wk", "L0_attn_Wv", "L0_attn_Wpost", "L0_attn_Wrel"]
        wnat = sb("wnat", [P, 5, P], ctx=ctx)
        pos = sb("pos", [NPOS, P], ctx=ctx)
        pds = sb("pds", [P, 6], ctx=ctx)
        wqs = sb("wqs", [P, P], ctx=ctx)
        wrelT = sb("wrelT", [P, P], ctx=ctx)
        posT = sb("posT", [P, NPOS], ctx=ctx)
        relT = sb("relT", [P, NPOS], ctx=ctx)
        relE = sb("relE", [P, CH, NPOS], ctx=ctx)
        wqkv = sb("cwqkv", [P, 3 * P], ctx=ctx)
        wqr = sb("wqr", [P, CH * NPOS], ctx=ctx)
        wpostT = sb("wpostT", [P, P], ctx=ctx)
        clear()
        with nc.Block(no_gpsimd_drain=True) as block:
            @block.sync
            def _(sp):
                for i, n in enumerate(names):
                    sp.dma_start(wnat[:, i, :], t[n]).then_inc(d_w, 16)
                sp.dma_start(pos[:], t["L0_attn_position_embeddings"]).then_inc(d_w, 16)
                for h in range(CH):
                    sp.dma_start(pds[h * CD:(h + 1) * CD, 0:1],
                                 t["L0_attn_per_dim_scale"].rearrange("(d o) -> d o", o=1)).then_inc(d_w, 16)

            @block.vector
            def _(dve):
                dve.wait_ge(d_w, 16 * (6 + CH))
                nc.vector.scalar_tensor_tensor(out=pds[:, 1:2], in0=pds[:, 0:1], scalar=-1.0, in1=pds[:, 0:1],
                                               op0=ALU.mult, op1=ALU.min).then_inc(s_sp, 1)
                dve.wait_ge(s_sp, 2)
                nc.vector.tensor_scalar(pds[:, 3:4], pds[:, 2:3], 1.0, None, ALU.add).then_inc(s_sp, 1)
                dve.wait_ge(s_sp, 4)
                nc.vector.scalar_tensor_tensor(out=pds[:, 5:6], in0=pds[:, 0:1], scalar=0.0, in1=pds[:, 4:5],
                                               op0=ALU.max, op1=ALU.add).then_inc(s_sp, 1)
                dve.wait_ge(s_sp, 5)
                nc.vector.tensor_scalar(wqs[:], wnat[:, 0, :], pds[:, 5:6], Q_SCALE,
                                        ALU.mult, ALU.mult).then_inc(s_ws, 1)
                dve.wait_ge(s_wt, 7)
                nc.vector.tensor_copy(relT[:], ps[:, 6, 0:NPOS]).then_inc(s_re, 1)
                dve.wait_ge(s_re, 1)
                nc.vector.tensor_tensor(relE[:], relT[:].unsqueeze(1).broadcast_to([P, CH, NPOS]),
                                        con[:, C_HM:C_HM + CH].unsqueeze(2).broadcast_to([P, CH, NPOS]),
                                        ALU.mult).then_inc(s_re, 1)
                dve.wait_ge(s_wt, 8)
                nc.vector.tensor_copy(wqr[:], ps[:, 7, 0:CH * NPOS]).then_inc(s_re, 1)

            @block.scalar
            def _(act):
                act.wait_ge(s_sp, 1)
                nc.scalar.activation(pds[:, 2:3], pds[:, 1:2], ACT.Exp).then_inc(s_sp, 1)
                act.wait_ge(s_sp, 3)
                nc.scalar.activation(pds[:, 4:5], pds[:, 3:4], ACT.Ln).then_inc(s_sp, 1)
                act.wait_ge(s_wt, 6)
                nc.scalar.copy(wqkv[:, 0:P], ps[:, 0, 0:P]).then_inc(s_we, 1)
                nc.scalar.mul(wqkv[:, P:2 * P], ps[:, 1, 0:P], K_SCALE).then_inc(s_we, 1)
                nc.scalar.copy(wqkv[:, 2 * P:], ps[:, 2, 0:P]).then_inc(s_we, 1)
                nc.scalar.copy(wpostT[:], ps[:, 3, 0:P]).then_inc(s_we, 1)
                nc.scalar.copy(wrelT[:], ps[:, 4, 0:P]).then_inc(s_we, 1)
                nc.scalar.copy(posT[:], ps[:, 5, 0:NPOS]).then_inc(s_we, 1)

            @block.tensor
            def _(pe):
                pe.wait_ge(s_ws, 1)
                nc.tensor.transpose(ps[:, 0, 0:P], wqs[:], ident).then_inc(s_wt, 1)
                for i in range(1, 5):
                    nc.tensor.transpose(ps[:, i, 0:P], wnat[:, i, :], ident).then_inc(s_wt, 1)
                nc.tensor.transpose(ps[:, 5, 0:NPOS], pos[:], ident[0:NPOS, 0:NPOS]).then_inc(s_wt, 1)
                pe.wait_ge(s_we, 6)
                nc.tensor.matmul(ps[:, 6, 0:NPOS], wrelT[:], posT[:], start=True, stop=True).then_inc(s_wt, 1)
                pe.wait_ge(s_re, 2)
                nc.tensor.matmul(ps[:, 7, 0:CH * NPOS], wqs[:], relE[:].rearrange("p h r -> p (h r)"),
                                 start=True, stop=True).then_inc(s_wt, 1)
        clear()

        ct = sb("ct", [P, CCH + TW], ctx=ctx)
        pm = sb("pm", [P, 1], ctx=ctx)
        qb = sb("qb", [P, CCH, P], ctx=ctx)
        kv = sb("kv", [P, CTX, 2, P], ctx=ctx)
        rel = sb("rel", [P, CH, CCH * NPOS], ctx=ctx)
        sc = sb("sc", [P, CH, CCH, CTX], ctx=ctx)
        NPR = 4
        prod = sb("prod", [P, NPR, CH * CTX * CD], ctx=ctx)
        sm = sb("sm", [P, CH * CCH], ctx=ctx)
        ri = sb("ri", [P, CH * CCH], ctx=ctx)
        ob = sb("ob", [P, CCH, P], ctx=ctx)
        obT = sb("obT", [P, CCH, P], ctx=ctx)
        so = sb("so", [P, P, CCH], ctx=ctx)
        s_ct, s_pj, s_ev, s_ed, s_mul, s_red, s_sc, s_sm, s_ot, s_oe, s_wp, s_so = (
            sem("s_ct"), sem("s_pj"), sem("s_ev"), sem("s_ed"), sem("s_mul"), sem("s_red"), sem("s_sc"),
            sem("s_sm"), sem("s_ot"), sem("s_oe"), sem("s_wp"), sem("s_so"))
        s_mulp, s_tanh, s_exp, s_on = sem("s_mulp"), sem("s_tanh"), sem("s_exp"), sem("s_on")

        def key_product(eng, c):
            return eng.tensor_tensor(
                prod[:, c % NPR, :].rearrange("p (h k d) -> p h k d", h=CH, k=CTX),
                qb[:, c, :].rearrange("p (h d) -> p h d", h=CH).unsqueeze(2).broadcast_to([P, CH, CTX, CD]),
                kv[:, :, 0, :].rearrange("p k (h d) -> p h k d", h=CH), ALU.mult)

        def value_product(eng, c):
            return eng.tensor_tensor(
                prod[:, c % NPR, :].rearrange("p (h d k) -> p h d k", h=CH, d=CD),
                sc[:, :, c, :].unsqueeze(2).broadcast_to([P, CH, CD, CTX]),
                kv[:, :, 1, :].rearrange("p k (h d) -> p h d k", h=CH), ALU.mult)

        def on_pool(c):
            return c % 3 != 0

        def pool_products(c):
            return sum(on_pool(j) for j in range(c + 1))

        half = CCH // 2
        halves = [sc[:, :, half * g:half * (g + 1), :] for g in range(2)]

        with nc.Fori(0, NTILE) as n:
            with nc.Block(no_gpsimd_drain=True) as block:
                @block.scalar
                def _(act):
                    nc.scalar.copy(ct[:], cx[:, bass.ds(n * TW, CCH + TW)]).then_inc(s_ct, 1)
                    for c in range(CCH):
                        act.wait_ge(s_pj, 3 * c + 1)
                        nc.scalar.copy(qb[:, c, :], ps[:, 3 * c % 6, 0:P])
                        nc.scalar.copy(kv[:, CCH + c, :, :].rearrange("p a d -> p (a d)"),
                                       ps[:, 3 * c % 6, P:3 * P]).then_inc(s_ev, 1)
                    for g in range(2):
                        act.wait_ge(s_sc, g + 1)
                        nc.scalar.activation(halves[g], halves[g], ACT.Tanh, scale=1.0 / SOFTCAP).then_inc(s_tanh, 1)
                        act.wait_ge(s_tanh, g + 1)
                        nc.scalar.activation(halves[g], halves[g], ACT.Exp, scale=SOFTCAP).then_inc(s_exp, 1)
                    for g in range(3):
                        act.wait_ge(s_ot, g + 1)
                        nc.scalar.copy(obT[:, 4 * g:4 * g + 4, :], ps[:, g, :].rearrange("p (c m) -> p c m", c=4)) \
                           .then_inc(s_oe, 1)
                    for g in range(3):
                        act.wait_ge(s_wp, g + 1)
                        nc.scalar.copy(so[:].rearrange("p m c -> p c m")[:, 4 * g:4 * g + 4, :],
                                       ps[:, 3 + g, :].rearrange("p (c m) -> p c m", c=4)).then_inc(s_so, 1)
                    act.wait_ge(s_so, 3)
                    act.dma_start(sT[:, bass.ds(n * TW, TW)], so[:].rearrange("p m c -> p (m c)")).then_inc(d_st, 16)
                    act.wait_ge(d_st, 16)

                @block.tensor
                def _(pe):
                    pe.wait_ge(s_ct, 1)
                    for c in range(CCH):
                        own = ct[:, CCH + c:CCH + c + (P - 1) * CCH + 1:CCH]
                        prev = ct[:, c:c + (P - 1) * CCH + 1:CCH]
                        if c >= 2:
                            pe.wait_ge(s_ev, c - 1)
                            pe.wait_ge(s_ed, 2 * (c - 1))
                        k = 3 * c % 6
                        nc.tensor.matmul(ps[:, k, 0:3 * P], own, wqkv[:], start=True, stop=True).then_inc(s_pj, 1)
                        nc.tensor.matmul(ps[:, k + 1, 0:CH * NPOS], own, wqr[:],
                                         start=True, stop=True).then_inc(s_pj, 1)
                        nc.tensor.matmul(ps[:, k + 2, 0:2 * P], prev, wqkv[:, P:],
                                         start=True, stop=True).then_inc(s_pj, 1)
                    pe.wait_ge(s_ev, CCH)
                    pe.wait_ge(s_ed, 2 * CCH)
                    for g in range(3):
                        pe.wait_ge(s_on, g + 1)
                        for c in range(4):
                            last = nc.tensor.transpose(ps[:, g, c * P:(c + 1) * P], ob[:, 4 * g + c, :], ident)
                        last.then_inc(s_ot, 1)
                    for g in range(3):
                        pe.wait_ge(s_oe, g + 1)
                        nc.tensor.matmul(ps[:, 3 + g, :], wpostT[:],
                                         obT[:, 4 * g:4 * g + 4, :].rearrange("p c m -> p (c m)"),
                                         start=True, stop=True).then_inc(s_wp, 1)

                @block.gpsimd
                def _(pool):
                    pool.wait_ge(s_ev, CCH)
                    pool.wait_ge(s_ed, 2 * CCH)
                    for c in range(CCH):
                        if on_pool(c):
                            if c >= NPR:
                                pool.wait_ge(s_red, c - NPR + 1)
                            key_product(nc.gpsimd, c).then_inc(s_mulp, 1)
                    for c in range(CCH):
                        if on_pool(c):
                            pool.wait_ge(s_exp, 1 + c // half)
                            pool.wait_ge(s_red, CCH + c - NPR + 1)
                            value_product(nc.gpsimd, c).then_inc(s_mulp, 1)

                @block.vector
                def _(dve):
                    nc.vector.tensor_copy(pm[:], con[:, bass.ds(n + C_PM, 1)]).then_inc(s_mul, 1)
                    dve.wait_ge(s_mul, 1)
                    for c in range(CCH):
                        k = 3 * c % 6
                        dve.wait_ge(s_pj, 3 * c + 2)
                        nc.vector.tensor_copy(rel[:, :, c * NPOS:(c + 1) * NPOS],
                                              ps[:, k + 1, 0:CH * NPOS].rearrange("p (h r) -> p h r", h=CH)) \
                            .then_inc(s_ed, 1)
                        dve.wait_ge(s_pj, 3 * c + 3)
                        nc.vector.tensor_scalar(kv[:, c, :, :].rearrange("p a d -> p (a d)"),
                                                ps[:, k + 2, 0:2 * P], pm[:], None, ALU.mult).then_inc(s_ed, 1)
                    dve.wait_ge(s_ev, CCH)
                    dve.wait_ge(s_ed, 2 * CCH)
                    done = 1

                    def sums(c, view, dst):
                        nonlocal done
                        if not on_pool(c):
                            dve.wait_ge(s_mul, done)
                        nc.vector.tensor_reduce(dst, prod[:, c % NPR, :].rearrange(view, h=CH, i=dst.shape[2]),
                                                AX_X, ALU.add).then_inc(s_red, 1)

                    sm3 = sm[:].rearrange("p (h c) -> p h c", h=CH)
                    ri3 = ri[:].rearrange("p (h c) -> p h c", h=CH)

                    def row_sums(g):
                        part = slice(half * g, half * g + half)
                        dve.wait_ge(s_exp, g + 1)
                        nc.vector.tensor_reduce(sm3[:, :, part], halves[g], AX_X, ALU.add).then_inc(s_sm, 1)
                        dve.wait_ge(s_sm, 2 * g + 1)
                        nc.vector.reciprocal(ri3[:, :, part], sm3[:, :, part]).then_inc(s_sm, 1)

                    for c in range(CCH):
                        if on_pool(c):
                            dve.wait_ge(s_mulp, pool_products(c))
                        else:
                            if c >= NPR:
                                dve.wait_ge(s_red, c - NPR + 1)
                            key_product(nc.vector, c).then_inc(s_mul, 1)
                            done += 1
                        sums(c, "p (h i d) -> p h i d", sc[:, :, c, :])
                        if c % half == half - 1:
                            g = c // half
                            dve.wait_ge(s_red, c + 1)
                            nc.vector.tensor_tensor(
                                halves[g], halves[g],
                                rel[:, :, g * half * CTX:(g + 1) * half * CTX]
                                .rearrange("p h (c k) -> p h c k", c=half),
                                ALU.add).then_inc(s_sc, 1)
                    row_sums(0)
                    for c in range(CCH):
                        if on_pool(c):
                            dve.wait_ge(s_mulp, pool_products(CCH - 1) + pool_products(c))
                        else:
                            dve.wait_ge(s_exp, 1 + c // half)
                            dve.wait_ge(s_red, CCH + c - NPR + 1)
                            value_product(nc.vector, c).then_inc(s_mul, 1)
                            done += 1
                        sums(c, "p (h i k) -> p h i k", ob[:, c, :].rearrange("p (h d) -> p h d", h=CH))
                        if c % 4 == 3:
                            g = c // 4
                            dve.wait_ge(s_red, CCH + c + 1)
                            o4 = ob[:, 4 * g:4 * g + 4, :].rearrange("p c (h d) -> p c h d", h=CH)
                            dve.wait_ge(s_sm, 2 if g == 0 else 4)
                            nc.vector.tensor_tensor(
                                o4, o4, ri3.rearrange("p h c -> p c h")[:, 4 * g:4 * g + 4, :].unsqueeze(3)
                                .broadcast_to([P, 4, CH, CD]), ALU.mult).then_inc(s_on, 1)
                        if c == half - 1:
                            row_sums(1)
            clear()


def transformer(nc, t, ctx, sb0, sem, clear, con, ident, ps, xT, d_raw, d_ff):
    def sb(name, shape, dt=F32):
        return sb0(name, shape, dt, ctx=ctx)

    raw = sb("raw", [P, 3 * INNER])
    wh, wl = sb("wh", [P, 3 * INNER], F32R), sb("wl", [P, 3 * INNER], F32R)
    sh, sl = sb("sh", [P, 2 * INNER], F32R), sb("sl", [P, 2 * INNER], F32R)
    wo = sb("wo", [P, HP, D])
    w1h, w1l = sb("w1h", [P, 2 * DI], F32R), sb("w1l", [P, 2 * DI], F32R)
    w2 = sb("w2", [P, NJ, D])
    svec = sb("svec", [P, DEPTH, 4])
    vecs = sb("vecs", [P, DEPTH, 2 + 2 * NJ + 1])
    vec = sb("vec", [P, 2 + 2 * NJ + 1])
    V_G, V_B, V_B1, V_B2 = 0, 1, 2, 2 + 2 * NJ
    scales = sb("scales", [P, 4])
    R_W1 = D * HP
    R_W2 = R_W1 + 2 * DI
    tab = sb("tab", [P, 4, S])
    maskb = sb("maskb", [P, 256], BF16)
    identb = sb("identb", [P, P], BF16)
    pairr = sb("pairr", [P, P], F32R)
    pairb = sb("pairb", [P, P], BF16)
    xhs, xls = sb("xhs", [P, 2, S], F32R), sb("xls", [P, 2, S], F32R)
    v = sb("v", [P, 2, TB, INNER])
    sq = sb("sq", [P, 2, S])
    sqlo = sb("sqlo", [P, 2, S], F32R)
    r1 = sb("r1", [P, 2, S])
    ra = sb("ra", [P, 2, S])
    rb = sb("rb", [P, 2, S])
    qn = sb("qn", [P, 2, S])
    kn = sb("kn", [P, 2, WIN + S])
    pr = sb("pr", [P, 2, S])
    stat = sb("stt", [P, 2, 3, 8])
    pt = sb("pt", [P, 2, S])
    on = sb("on", [P, S])
    oT = sb("oT", [P, HP, S])
    fx = sb("fx", [P, S])
    fc = sb("fc", [P, S])
    fq = sb("fq", [P, S])
    fr = sb("fr", [P, S])
    fh, fl = sb("fh", [P, S], F32R), sb("fl", [P, S], F32R)
    gx = sb("gx", [P, NJ, S])

    d_w = sem("d_lw")
    s_set, s_hi, s_lo, s_vz, d_vec = sem("s_set"), sem("t_hi"), sem("t_lo"), sem("s_vz"), sem("d_vec")
    s_w = sem("s_w")
    names = ("xh v vev ab sq sl rot g ssq r ln add qkn S m sub exp rs ri pt ptev o oev ot otev wo x1 "
             "fx mean fc fq var fe fr fn fh fl w1 gx gl h w2 x2 shifted cleared").split()
    sets = [{n: sem(f"r{k}_{n}") for n in names} for k in range(2)]
    A, BB, SS, S0, S1, TT, O0, O1 = range(8)
    swapped = raw[:, 0:2 * INNER].rearrange("p (h t d) -> p h t d", t=2, d=HALF)

    def shift_parts(act, dve, slot, hi, lo, s_hi, s_lo):
        if act:
            nc.scalar.copy(hi[0:64, :], xT[0:64, slot, :]).then_inc(s_hi, 1)
            nc.scalar.copy(hi[64:128, 1:], xT[64:128, slot, 0:S - 1]).then_inc(s_hi, 1)
        if dve:
            dve.wait_ge(s_hi, 2)
            nc.vector.tensor_tensor(lo[0:64, :], xT[0:64, slot, :], hi[0:64, :].bitcast(F32),
                                    ALU.subtract).then_inc(s_lo, 1)
            nc.vector.tensor_tensor(lo[64:128, 1:], xT[64:128, slot, 0:S - 1], hi[64:128, 1:].bitcast(F32),
                                    ALU.subtract).then_inc(s_lo, 1)

    clear()
    with nc.Block(no_gpsimd_drain=True) as block:
        @block.sync
        def _(sp):
            sp.dma_start(raw[:], t["L0_ffn_Wqkv"][0]).then_inc(d_raw, 16)
            for i, n in ((0, "L0_ffn_q_scale"), (2, "L0_ffn_k_scale")):
                src = t[n].rearrange("l (d o) -> d l o", o=1)
                for g in range(4):
                    own, other = (g % 2) * HALF, (1 - g % 2) * HALF
                    sp.dma_start(svec[g * HALF:(g + 1) * HALF, :, i:i + 1], src[own:own + HALF],
                                 allow_slow_non_contiguous=True).then_inc(d_w, 16)
                    sp.dma_start(svec[g * HALF:(g + 1) * HALF, :, i + 1:i + 2],
                                 src[other:other + HALF], allow_slow_non_contiguous=True).then_inc(d_w, 16)
            sp.wait_ge(d_w, 16 * 16)

        @block.scalar
        def _(act):
            act.wait_ge(s_vz, 1)
            for i, n in ((V_G, "L0_ffn_ln_g"), (V_B, "L0_ffn_ln_b"), (V_B2, "L0_ffn_b2")):
                act.dma_start(vecs[:, :, i:i + 1], t[n].rearrange("l (d o) -> d l o", o=1),
                              allow_slow_non_contiguous=True).then_inc(d_vec, 16)
            b1 = t["L0_ffn_b1"].rearrange("l (d o) -> d l o", o=1)
            for a in range(2):
                for j in range(NJ):
                    o = a * DI + j * P
                    c = V_B1 + a * NJ + j
                    act.dma_start(vecs[0:JW[j], :, c:c + 1], b1[o:o + JW[j]],
                                  allow_slow_non_contiguous=True).then_inc(d_vec, 16)
            act.wait_ge(d_vec, 16 * (3 + 2 * NJ))

        @block.gpsimd
        def _(pool):
            zeros = (wo[:], w2[:], vec[:], v[:, 1], qn[:], kn[:], pt[:])
            for z in zeros:
                nc.gpsimd.memset(z, 0.0).then_inc(s_set, 1)
            for z in (w1h, w1l, xhs, xls):
                nc.gpsimd.memset(z[:].bitcast(F32), 0.0).then_inc(s_set, 1)
            for z in (pr, r1, stat):
                nc.gpsimd.memset(z[:], 1.0).then_inc(s_set, 1)
            pool.wait_ge(s_set, len(zeros) + 7)

        @block.vector
        def _(dve):
            nc.vector.memset(vecs[:], 0.0).then_inc(s_vz, 1)
            nc.vector.memset(v[:, 0], 0.0).then_inc(s_vz, 1)
            nc.vector.memset(oT[:], 0.0).then_inc(s_vz, 1)
            nc.vector.memset(fx[:], 0.0).then_inc(s_hi, 1)
            nc.vector.memset(gx[:], 0.0).then_inc(s_hi, 1)
            nc.vector.memset(xT[:, B, :], 0.0).then_inc(s_hi, 1)
            nc.vector.tensor_copy(maskb[:], con[:, C_MASK:C_MASK + 256]).then_inc(s_hi, 1)
            nc.vector.tensor_copy(identb[:], ident).then_inc(s_hi, 1)
            nc.vector.tensor_copy(pairr[:], con[:, C_PAIR:C_PAIR + P]).then_inc(s_hi, 1)
            nc.vector.tensor_copy(pairb[:], con[:, C_PAIR:C_PAIR + P]).then_inc(s_hi, 1)
            dve.wait_ge(s_hi, 7)
            dve.wait_ge(s_vz, 3)
    clear()
    with nc.Block(no_gpsimd_drain=True) as block:
        @block.scalar
        def _(act):
            shift_parts(act, None, 0, xhs[:, 0], xls[:, 0], s_hi, s_lo)

        @block.vector
        def _(dve):
            shift_parts(None, dve, 0, xhs[:, 0], xls[:, 0], s_hi, s_lo)
            dve.wait_ge(s_lo, 2)
    clear()

    def attention_weights(l):
        with nc.Block(no_gpsimd_drain=True) as block:
            @block.sync
            def _(sp):
                sp.dma_start(tab[:], t["rotary"]).then_inc(d_w, 16)
                sp.wait_ge(s_lo, 3)
                sp.dma_start(raw[:, 0:R_W1].rearrange("p (a n) -> p a n", a=HP),
                             t["L0_ffn_Wo"][l].rearrange("(a p) n -> p a n", p=P)).then_inc(d_ff, 16)
                sp.dma_start(raw[:, R_W1:R_W2], t["L0_ffn_W1"][l]).then_inc(d_ff, 16)
                for j in range(NJ):
                    sp.dma_start(raw[0:JW[j], R_W2 + j * D:R_W2 + (j + 1) * D],
                                 t["L0_ffn_W2"][l, j * P:j * P + JW[j], :]).then_inc(d_ff, 16)

            @block.scalar
            def _(act):
                act.wait_ge(d_raw, 16)
                nc.scalar.copy(wh[:], raw[:]).then_inc(s_hi, 1)
                for a in range(2):
                    nc.scalar.copy(sh[:].rearrange("p (h t d) -> p h t d", t=2, d=HALF)[:, :, a, :],
                                   swapped[:, :, 1 - a, :]).then_inc(s_hi, 1)

            @block.vector
            def _(dve):
                dve.wait_ge(s_hi, 1)
                nc.vector.tensor_tensor(wl[:], raw[:], wh[:].bitcast(F32), ALU.subtract).then_inc(s_lo, 1)
                dve.wait_ge(s_hi, 3)
                for a in range(2):
                    nc.vector.tensor_tensor(
                        sl[:].rearrange("p (h t d) -> p h t d", t=2, d=HALF)[:, :, a, :], swapped[:, :, 1 - a, :],
                        sh[:].bitcast(F32).rearrange("p (h t d) -> p h t d", t=2, d=HALF)[:, :, a, :],
                        ALU.subtract).then_inc(s_lo, 1)
                nc.vector.tensor_copy(scales[:], svec[:, l, :]).then_inc(s_lo, 1)
                dve.wait_ge(s_lo, 4)
                dve.wait_ge(d_w, 16)
                for i in range(4):
                    nc.vector.tensor_scalar(tab[:, i, :], tab[:, i, :], scales[:, i:i + 1], None,
                                            ALU.mult).then_inc(s_lo, 1)
                dve.wait_ge(s_lo, 8)
        nc.sync.sem_clear(d_raw)
        clear()

    def feed_forward_weights(l):
        w1raw = raw[:, R_W1:R_W2]
        with nc.Block(no_gpsimd_drain=True) as block:
            @block.sync
            def _(sp):
                sp.wait_ge(s_hi, 1 + NJ)
                sp.wait_ge(s_lo, 1)
                sp.dma_start(raw[:], t["L0_ffn_Wqkv"][(l + 1) % DEPTH]).then_inc(d_raw, 16)

            @block.scalar
            def _(act):
                act.wait_ge(d_ff, 16 * (2 + NJ))
                nc.scalar.copy(w1h[:], w1raw).then_inc(s_hi, 1)
                for j in range(NJ):
                    nc.scalar.copy(w2[0:JW[j], j, :], raw[0:JW[j], R_W2 + j * D:R_W2 + (j + 1) * D]).then_inc(s_hi, 1)

            @block.vector
            def _(dve):
                nc.vector.tensor_copy(vec[:], vecs[:, l, :]).then_inc(s_w, 1)
                dve.wait_ge(d_ff, 16 * (2 + NJ))
                nc.vector.tensor_copy(wo[:].rearrange("p a n -> p (a n)"), raw[:, 0:R_W1]).then_inc(s_w, 1)
                dve.wait_ge(s_hi, 1)
                dve.wait_ge(s_w, 2)
                nc.vector.tensor_tensor(w1l[:], w1raw, w1h[:].bitcast(F32), ALU.subtract).then_inc(s_lo, 1)
        nc.sync.sem_clear(d_ff)
        clear()

    V_AT = [(0, 0, SS), (0, 1, O0), (1, 0, SS), (2, 0, SS), (3, 0, O1), (4, 0, SS), (4, 0, O1), (5, 1, O0)]

    def round_(k, follows, half, pb, nb, drain=False):
        full = not drain

        def live(i, lag):
            return full or i < lag

        def before(i, lag):
            return i if full else min(i, lag)

        cur, other = sets[k], sets[1 - k]
        xh, xl = xhs[:, half], xls[:, half]
        next_xh, next_xl = xhs[:, 1 - half], xls[:, 1 - half]
        counts = {**dict.fromkeys("rot g ssq add qkn".split(), 2 * HP),
                  **dict.fromkeys("oev ptev otev sub o S ri ot pt".split(), HP), "xh": 4}

        def after(eng, name, n):
            if n > 0:
                eng.wait_ge(cur[name], n)
            elif follows:
                eng.wait_ge(other[name], counts[name] + n)

        def begin(eng):
            if follows:
                eng.wait_ge(other["cleared"], 1)

        def v_chunks(i, end):
            return [j for j in range(8) if full and V_AT[j][:2] == (i, end)]

        def tensor(pe):
            begin(pe)

            def three(dst, ah, al, bh, bl):
                nc.tensor.matmul(dst, al, bh, start=True, stop=False)
                nc.tensor.matmul(dst, ah, bl, start=False, stop=False)
                return nc.tensor.matmul(dst, ah, bh, start=False, stop=True)

            def project(i, k):
                after(pe, "rot", 2 * i + k)
                if (i, k) == (0, 0):
                    after(pe, "xh", 0)
                c = k * INNER + i * P
                three(ps[:, A, :], wh[:, c:c + P], wl[:, c:c + P], xh, xl)
                three(ps[:, BB, :], sh[:, c:c + P], sl[:, c:c + P], xh, xl).then_inc(cur["ab"], 1)

            def squares(i, k):
                pe.wait_ge(cur["sl"], 2 * i + k + 1)
                after(pe, "g", 2 * i + k)
                nc.tensor.matmul(ps[:, SS, :], pairr[:], sqlo[:, k, :], start=True, stop=False)
                nc.tensor.matmul(ps[:, SS, :], pairb[:], sq[:, k, :].bitcast(BF16)[:, 1::2],
                                 start=False, stop=True).then_inc(cur["ssq"], 1)

            def values_of(j):
                hf, tb, bank = j // 4, j % 4, V_AT[j][2]
                c = 2 * INNER + 512 * hf
                three(ps[:, bank, :], xh[:, tb * P:(tb + 1) * P], xl[:, tb * P:(tb + 1) * P],
                      wh[:, c:c + 512], wl[:, c:c + 512]).then_inc(cur["v"], 1)

            def scores(i):
                after(pe, "sub", before(i, 1))
                for e in range(2):
                    nc.tensor.matmul(ps[:, S0 + e, 0:256], identb[:], maskb[:], start=True, stop=False,
                                     skip_group_check=True)
                pe.wait_ge(cur["qkn"], 2 * i + 1)
                for e in range(2):
                    q = qn[e * DH:(e + 1) * DH, (i - 1) % 2, :]
                    k = kn[e * DH:(e + 1) * DH, (i - 1) % 2, :]
                    for wd in range(S // WIN):
                        tb, whi, wlo = wd // 4, wd // 2 % 2, wd % 2
                        strip = (tb % 2 * 2 + wlo) * WIN
                        col = (tb // 2 * 2 + whi) * 2 * WIN
                        last = nc.tensor.matmul(
                            ps[strip:strip + WIN, S0 + e, col:col + 2 * WIN], q[:, wd * WIN:(wd + 1) * WIN],
                            k[:, wd * WIN:(wd + 2) * WIN], start=False, stop=True, skip_group_check=True,
                            tile_position=(e * DH, strip))
                last.then_inc(cur["S"], 1)

            def turn_probs(i):
                pe.wait_ge(cur["exp"], i + 1)
                after(pe, "otev", i)
                for m in range(4):
                    last = nc.tensor.transpose(ps[:, TT, m * P:(m + 1) * P],
                                               pr[:, i % 2, m * P:(m + 1) * P], ident)
                last.then_inc(cur["pt"], 1)

            def values(i):
                after(pe, "ptev", i)
                after(pe, "oev", i)
                if full and i in (3, 7):
                    pe.wait_ge(cur["vev"], i + 1)
                    pe.wait_ge(cur["shifted"], 32 if i == 3 else 64)
                filled = {1: (("vev", 2), ()), 3: (("x1", 1), ("vev", 5)), 4: (("fe", 1), ("vev", 7)),
                          5: (("gx", 1), ("gx", 2)), 6: (("vev", 8), ("h", 1)), 7: (("h", 3), ())}
                hp = (i - 3) % HP
                for whi in range(2):
                    if full and i in filled and filled[i][whi]:
                        reader, n = filled[i][whi]
                        pe.wait_ge(cur[reader], n)
                    for tb in range(TB):
                        for wlo in range(2):
                            for e in range(2):
                                strip = (tb % 2 * 2 + wlo) * WIN
                                c = (e * 2 + tb // 2) * P + strip
                                o = (tb // 2) * P + e * DH
                                hh = 2 * hp + e
                                last = nc.tensor.matmul(
                                    ps[strip:strip + WIN, O0 + whi, o:o + DH],
                                    pt[whi * DH:(whi + 1) * DH, (i - 1) % 2, c:c + WIN],
                                    v[whi * DH:(whi + 1) * DH, 1 - wlo, tb, hh * DH:(hh + 1) * DH],
                                    start=True, stop=True, skip_group_check=True,
                                    tile_position=(whi * DH, strip))
                last.then_inc(cur["o"], 1)

            def turn_out(i):
                pe.wait_ge(cur["oev"], i + 1)
                pe.wait_ge(cur["ptev"], before(i + 1, 2))
                after(pe, "otev", i)
                for m in range(4):
                    last = nc.tensor.transpose(ps[:, TT, m * P:(m + 1) * P], on[:, m * P:(m + 1) * P], ident)
                last.then_inc(cur["ot"], 1)

            def up(a, j, bank):
                c = a * DI + j * P
                three(ps[0:JW[j], bank, :], w1h[:, c:c + JW[j]], w1l[:, c:c + JW[j]], fh[:], fl[:]) \
                    .then_inc(cur["w1"], 1)

            def middle(i):
                after(pe, "oev", before(i, 3))
                if full:
                    after(pe, "g", 2 * i)
                for j in v_chunks(i, 0):
                    values_of(j)
                if i == 3:
                    pe.wait_ge(cur["fx"], 2)
                    nc.tensor.matmul(ps[:, SS, :], con[:, C_MEAN:C_MEAN + P], fx[:], start=True,
                                     stop=True).then_inc(cur["mean"], 1)
                if i == 5:
                    pe.wait_ge(cur["fc"], 1)
                    up(1, 2, O1)
                    up(1, 1, SS)
                if i == 6:
                    pe.wait_ge(cur["gx"], 3)
                    up(0, 1, O1)
                    up(0, 0, SS)
                if i == 7:
                    pe.wait_ge(cur["h"], 3)
                    for j in range(NJ):
                        last = nc.tensor.matmul(ps[:, SS, :], w2[0:JW[j], j, :], gx[0:JW[j], j, :],
                                                start=(j == 0), stop=(j == NJ - 1))
                    last.then_inc(cur["w2"], 1)

            def end(i):
                for j in v_chunks(i, 1):
                    values_of(j)
                if i == 2:
                    pe.wait_ge(cur["otev"], 2)
                    for p in range(HP):
                        if p == HP - 1:
                            pe.wait_ge(cur["otev"], 3)
                        last = nc.tensor.matmul(ps[:, O0, :], wo[:, p, :], oT[:, p, :], start=(p == 0),
                                                stop=(p == HP - 1))
                    last.then_inc(cur["wo"], 1)
                if i == 3:
                    pe.wait_ge(cur["fq"], 1)
                    nc.tensor.matmul(ps[:, O0, :], con[:, C_MEAN:C_MEAN + P], fq[:], start=True,
                                     stop=True).then_inc(cur["var"], 1)
                if i == 4:
                    pe.wait_ge(cur["fe"], 1)
                    pe.wait_ge(cur["fh"], 1)
                    pe.wait_ge(cur["fl"], 1)
                    up(1, 0, O0)
                if i == 6:
                    pe.wait_ge(cur["gx"], 1)
                    up(0, 2, O0)

            for i in range(HP):
                if full:
                    project(i, 0)
                middle(i)
                if live(i, 3):
                    values(i)
                if full:
                    project(i, 1)
                if live(i, 2):
                    turn_probs(i)
                if full:
                    reader, n = (("vev", 1), ("vev", 3), ("vev", 4), ("fc", 1), ("vev", 6), ("gx", 3), ("h", 2),
                                 ("x2", 1))[i]
                    pe.wait_ge(cur[reader], n)
                    squares(i, 0)
                if live(i, 1):
                    scores(i)
                if live(i, 3):
                    turn_out(i)
                if full:
                    squares(i, 1)
                end(i)

        def scalar(act):
            begin(act)
            nc.scalar.preload_act_table_set(LN_EXP)

            def square(i, k):
                act.wait_ge(cur["ab"], 2 * i + k + 1)
                after(act, "ssq", 2 * i + k - 1)
                nc.scalar.activation(sq[:, k, :], ps[:, A, :], ACT.Square).then_inc(cur["sq"], 1)

            def inverse_norm(i, k):
                n = 2 * i + 1 if k else 2 * i + 2
                after(act, "g", n - 1)
                nc.scalar.activation(r1[:, k, :], r1[:, k, :], ACT.Ln, scale=RN * RN).then_inc(cur["ln"], 1)
                act.wait_ge(cur["ln"], n)
                nc.scalar.activation(r1[:, k, :], r1[:, k, :], ACT.Exp, scale=-0.5).then_inc(cur["r"], 1)

            def values_read(j):
                act.wait_ge(cur["v"], j + 1)
                if j == 4:
                    act.wait_ge(cur["o"], 3)
                hf, tb = j // 4, j % 4
                nc.scalar.copy(v[:, 0, tb, hf * 512:(hf + 1) * 512], ps[:, V_AT[j][2], :]).then_inc(cur["vev"], 1)

            def gate(j, bank, n):
                m = JW[j]
                act.wait_ge(cur["w1"], n)
                nc.scalar.activation(gx[0:m, j, :], ps[0:m, bank, :], ACT.Identity,
                                     bias=vec[0:m, V_B1 + NJ + j:V_B1 + NJ + j + 1]).then_inc(cur["gx"], 1)

            for i in range(HP):
                if full:
                    square(i, 0)
                if i == 6:
                    nc.scalar.preload_act_table_set(LN_EXP)
                    if full:
                        inverse_norm(5, 0)
                if live(i, 2):
                    after(act, "sub", i)
                    nc.scalar.activation(pr[:, i % 2, :], pr[:, i % 2, :], ACT.Exp).then_inc(cur["exp"], 1)
                for j in v_chunks(i, 0):
                    values_read(j)
                if i == 5:
                    gate(2, O1, 2)
                    gate(1, SS, 3)
                if live(i, 1):
                    inverse_norm(i, 1)
                if i == 4:
                    act.wait_ge(cur["fe"], 1)
                    nc.scalar.activation(fr[:], fr[:], ACT.Ln).then_inc(cur["fr"], 1)
                    act.wait_ge(cur["fr"], 1)
                    nc.scalar.activation(fr[:], fr[:], ACT.Exp, scale=-0.5).then_inc(cur["fr"], 1)
                if i == 3:
                    act.wait_ge(cur["fc"], 1)
                    nc.scalar.activation(fq[:], fc[:], ACT.Square).then_inc(cur["fq"], 1)
                if full:
                    square(i, 1)
                if live(i, 2):
                    act.wait_ge(cur["pt"], i + 1)
                    after(act, "o", before(i, 3))
                    nc.scalar.copy(pt[:, i % 2, :], ps[:, TT, :]).then_inc(cur["ptev"], 1)
                if i == 4:
                    act.wait_ge(cur["fn"], 1)
                    nc.scalar.activation(fc[:], fc[:], ACT.Identity, scale=vec[:, V_G:V_G + 1],
                                         bias=vec[:, V_B:V_B + 1]).then_inc(cur["fn"], 1)
                    act.wait_ge(cur["fn"], 2)
                    nc.scalar.copy(fh[:], fc[:]).then_inc(cur["fh"], 1)
                if i == 5:
                    act.wait_ge(cur["gx"], NJ)
                    nc.scalar.activation(gx[:], gx[:], ACT.Gelu).then_inc(cur["gl"], 1)
                elif full:
                    inverse_norm(i, 0)
                if live(i, 3):
                    act.wait_ge(cur["ot"], i + 1)
                    nc.scalar.copy(oT_view(oT, (i - 3) % HP),
                                   ps[:, TT, :].rearrange("p (wh t2 t1 s) -> p wh t2 t1 s", wh=2, t2=2, t1=2)) \
                       .then_inc(cur["otev"], 1)
                if i == 2 and full:
                    shift_parts(act, None, nb, next_xh, next_xl, cur["xh"], None)
                for j in v_chunks(i, 1):
                    values_read(j)
                if i == 4:
                    gate(0, O0, 1)

        def gpsimd(pool):
            begin(pool)

            def rotate(i, k):
                n = 2 * i + k
                pool.wait_ge(cur["rot"], n + 1)
                after(pool, "S", i)
                dst = kn[:, i % 2, WIN:] if k else qn[:, i % 2, :]
                nc.gpsimd.tensor_tensor(dst, ra[:, k, :], rb[:, k, :], ALU.add).then_inc(cur["add"], 1)

            def normalise(i, k):
                dst = kn[:, (i - 1) % 2, WIN:] if k else qn[:, i % 2, :]
                after(pool, "add", 2 * i if k else 2 * i + 1)
                pool.wait_ge(cur["r"], 2 * i + 1 if k else 2 * i + 2)
                nc.gpsimd.tensor_tensor(dst, dst, r1[:, k, :], ALU.mult).then_inc(cur["qkn"], 1)

            for i in range(HP):
                if live(i, 1):
                    normalise(i, 1)
                if full:
                    rotate(i, 0)
                    rotate(i, 1)
                    normalise(i, 0)

        def sync(sp):
            for hf in range(2 if full else 0):
                c = slice(512 * hf, 512 * hf + 512)
                sp.wait_ge(cur["vev"], 4 * hf + 4)
                if hf:
                    sp.wait_ge(cur["o"], 3)
                sp.dma_start(v[WIN:P, 1, :, c], v[0:P - WIN, 0, :, c]).then_inc(cur["shifted"], 16)
                sp.dma_start(v[0:WIN, 1, 1:TB, c], v[P - WIN:P, 0, 0:TB - 1, c]).then_inc(cur["shifted"], 16)
                if not hf:
                    sp.wait_ge(cur["o"], 3)
                    sp.wait_ge(cur["otev"], 3)
                    sp.wait_ge(cur["oev"], 3)
                    sp.wait_ge(cur["qkn"], 5)
                    first, last = other["xh"].num, other["cleared"].num
                    sp.sem_clear(range(first, last + 1)).then_inc(cur["cleared"], 1)
            if full:
                sp.wait_ge(cur["shifted"], 64)

        def vector(dve):
            begin(dve)

            def rotary(i, k):
                after(dve, "add", 2 * i + k - 1)
                dve.wait_ge(cur["ab"], 2 * i + k + 1)
                nc.vector.tensor_tensor(rb[:, k, :], ps[:, BB, :], tab[:, 2 * k + 1, :], ALU.mult)
                dve.wait_ge(cur["sq"], 2 * i + k + 1)
                nc.vector.tensor_tensor(ra[:, k, :], ps[:, A, :], tab[:, 2 * k, :], ALU.mult).then_inc(cur["rot"], 1)
                after(dve, "ssq", 2 * i + k - 1)
                nc.vector.tensor_tensor(sqlo[:, k, :], sq[:, k, :], sq[:, k, :].bitcast(BF16)[:, 1::2],
                                        ALU.subtract).then_inc(cur["sl"], 1)

            def guard(i, k):
                dve.wait_ge(cur["ssq"], 2 * i + k + 1)
                after(dve, "qkn", 2 * i + k)
                nc.vector.tensor_scalar(r1[:, k, :], ps[:, SS, :], 1e-24, None, ALU.max).then_inc(cur["g"], 1)

            def subtract_max(i):
                b = (i - 1) % 2
                dve.wait_ge(cur["S"], i + 1)
                s4 = ps[:, S0:S1 + 1, 0:256].rearrange("p e (g k) -> p e g k", g=4)
                after(dve, "pt", before(i, 2))
                nc.vector.tensor_reduce(stat[:, b, 0, :].rearrange("p (e g) -> p e g", e=2), s4, AX_X,
                                        ALU.max).then_inc(cur["m"], 1)
                dve.wait_ge(cur["m"], i + 1)
                nc.vector.tensor_tensor(pr[:, b, :].rearrange("p (e g k) -> p e g k", e=2, g=4), s4,
                                        stat[:, b, 0, :].rearrange("p (e g) -> p e g", e=2).unsqueeze(3)
                                        .broadcast_to([P, 2, 4, 64]), ALU.subtract).then_inc(cur["sub"], 1)

            def outputs(i):
                dve.wait_ge(cur["o"], i + 1)
                after(dve, "ri", i)
                after(dve, "ot", i)
                nc.vector.tensor_tensor(
                    on[:].rearrange("p (w g d) -> p w g d", w=2, g=4),
                    ps[:, O0:O1 + 1, 0:256].rearrange("p w (g d) -> p w g d", g=4),
                    stat[:, (i - 1) % 2, 2, :].rearrange("p (w g) -> p w g", w=2).unsqueeze(3)
                    .broadcast_to([P, 2, 4, DH]), ALU.mult).then_inc(cur["oev"], 1)

            def row_sums(i):
                b = i % 2
                dve.wait_ge(cur["exp"], i + 1)
                nc.vector.tensor_reduce(stat[:, b, 1, :], pr[:, b, :].rearrange("p (g k) -> p g k", g=8),
                                        AX_X, ALU.add).then_inc(cur["rs"], 1)
                dve.wait_ge(cur["rs"], i + 1)
                nc.vector.reciprocal(
                    stat[:, b, 2, :].rearrange("p (w t e) -> p e t w", w=2, t=2),
                    stat[:, b, 1, :].rearrange("p (e t w) -> p e t w", e=2, t=2)).then_inc(cur["ri"], 1)

            def gated(j, bank, n):
                m = JW[j]
                dve.wait_ge(cur["gl"], 1)
                dve.wait_ge(cur["w1"], n)
                nc.vector.scalar_tensor_tensor(out=gx[0:m, j, :], in0=ps[0:m, bank, :],
                                               scalar=vec[0:m, V_B1 + j:V_B1 + j + 1], in1=gx[0:m, j, :],
                                               op0=ALU.add, op1=ALU.mult).then_inc(cur["h"], 1)

            for i in range(HP):
                if full:
                    rotary(i, 0)
                if i == 6:
                    gated(1, O1, NJ + 1)
                    gated(0, SS, NJ + 2)
                if i == 7:
                    dve.wait_ge(cur["w2"], 1)
                    nc.vector.scalar_tensor_tensor(out=xT[:, pb, :], in0=ps[:, SS, :],
                                                   scalar=vec[:, V_B2:V_B2 + 1], in1=xT[:, pb, :],
                                                   op0=ALU.add, op1=ALU.add).then_inc(cur["x2"], 1)
                if i == 3:
                    dve.wait_ge(cur["mean"], 1)
                    nc.vector.tensor_tensor(fc[:], fx[:], ps[:, SS, :], ALU.subtract).then_inc(cur["fc"], 1)
                if live(i, 3):
                    outputs(i)
                if i == 4:
                    dve.wait_ge(cur["fr"], 2)
                    nc.vector.tensor_tensor(fc[:], fc[:], fr[:], ALU.mult).then_inc(cur["fn"], 1)
                if full:
                    rotary(i, 1)
                    guard(i, 0)
                if i == 4:
                    dve.wait_ge(cur["fh"], 1)
                    nc.vector.tensor_tensor(fl[:], fc[:], fh[:].bitcast(F32), ALU.subtract).then_inc(cur["fl"], 1)
                if live(i, 2):
                    row_sums(i)
                if full:
                    guard(i, 1)
                if i == 6:
                    gated(2, O0, NJ + 3)
                if live(i, 1):
                    subtract_max(i)
                if i == 2 and full:
                    shift_parts(None, dve, nb, next_xh, next_xl, cur["xh"], cur["xh"])
                if i == 2:
                    dve.wait_ge(cur["wo"], 1)
                    nc.vector.tensor_tensor(xT[:, pb, :], ps[:, O0, :], xT[:, pb, :], ALU.add).then_inc(cur["x1"], 1)
                    dve.wait_ge(cur["x1"], 1)
                    nc.vector.tensor_copy(fx[0:64, :], xT[0:64, pb, :]).then_inc(cur["fx"], 1)
                    nc.vector.tensor_copy(fx[64:128, 1:], xT[64:128, pb, 0:S - 1]).then_inc(cur["fx"], 1)
                if i == 3:
                    dve.wait_ge(cur["var"], 1)
                    nc.vector.tensor_scalar(fr[:], ps[:, O0, :], EPS, None, ALU.add).then_inc(cur["fe"], 1)

        return dict(tensor=tensor, scalar=scalar, gpsimd=gpsimd, sync=sync, vector=vector)

    def lone_round(pb, nb, drain=False):
        r = round_(0, False, 0, pb, nb, drain)
        with nc.Block(no_gpsimd_drain=True) as block:
            block.tensor(r["tensor"])
            block.scalar(r["scalar"])
            block.sync(r["sync"])

            @block.gpsimd
            def _(pool):
                r["gpsimd"](pool)
                pool.wait_ge(sets[0]["qkn"], 1 if drain else 2 * HP)

            @block.vector
            def _(dve):
                r["vector"](dve)
                if not drain:
                    dve.wait_ge(sets[0]["xh"], 4)
                dve.wait_ge(sets[0]["x2"], 1)
        clear()

    def layer_rounds():
        def program(eng, of):
            of(round_(0, False, 1, 0, 2))(eng)
            with eng.Fori(0, (B - 2) // 2) as n:
                of(round_(1, True, 0, 2 * n + 1, 2 * n + 3))(eng)
                of(round_(0, True, 1, 2 * n + 2, (2 * n + 4) % B))(eng)

        with nc.Block(no_gpsimd_drain=True) as block:
            @block.tensor
            def _(pe):
                program(pe, lambda r: r["tensor"])

            @block.scalar
            def _(act):
                program(act, lambda r: r["scalar"])

            @block.gpsimd
            def _(pool):
                program(pool, lambda r: r["gpsimd"])
                pool.wait_ge(sets[0]["qkn"], 2 * HP)

            @block.sync
            def _(sp):
                program(sp, lambda r: r["sync"])

            @block.vector
            def _(dve):
                program(dve, lambda r: r["vector"])
                dve.wait_ge(sets[0]["xh"], 4)
                dve.wait_ge(sets[0]["x2"], 1)
        clear()

    with nc.Fori(0, DEPTH) as l:
        attention_weights(l)
        lone_round(B - 1 + ((B - l) >> 3), 1)
        feed_forward_weights(l)
        layer_rounds()
    lone_round(B - 1, None, drain=True)


def oT_view(oT, i):
    return oT[:, i, :].rearrange("p (t2 t1 wh s) -> p wh t2 t1 s", t2=2, t1=2, wh=2)


_INS = ['L0_attn_hidden_states', 'L0_attn_position_embeddings', 'L0_attn_Wq', 'L0_attn_Wk', 'L0_attn_Wv',
        'L0_attn_Wpost', 'L0_attn_Wrel', 'L0_attn_per_dim_scale', 'L0_ffn_Wqkv', 'L0_ffn_q_scale',
        'L0_ffn_k_scale', 'L0_ffn_Wo', 'L0_ffn_ln_g', 'L0_ffn_ln_b', 'L0_ffn_W1', 'L0_ffn_b1', 'L0_ffn_W2',
        'L0_ffn_b2']


def kernel(**inputs):
    import concourse.bacc as bacc
    from concourse.bass_utils import run_bass_kernel_spmd

    nc = bacc.Bacc("TRN2", target_bir_lowering=False, num_devices=1)
    arrays, args = {}, {}
    given = {**inputs, "consts": constants(), "rotary": rotary_tables()}
    for name in _INS + ["consts", "rotary"]:
        a = np.ascontiguousarray(given[name])
        arrays[f"in_{name}"] = a
        args[name] = nc.dram_tensor(f"in_{name}", a.shape, mybir.dt.from_np(a.dtype), kind="ExternalInput").ap()
    out = nc.dram_tensor("out_0", (B, S, D), F32, kind="ExternalOutput").ap()
    build(nc, args, out)
    r = run_bass_kernel_spmd(nc, [arrays], core_ids=[0])
    return r.results[0]["out_0"]
```
